# Optimizing a Trainium2 kernel written in Bass

```python
import numpy as np
import jax
import jax.numpy as jnp

def _softmax(x, axis=-1):
    return jax.nn.softmax(x, axis=axis)

def _gelu(x):
    return jax.nn.gelu(x, approximate=True)

def _silu(x):
    return jax.nn.silu(x)

def _sigmoid(x):
    return jax.nn.sigmoid(x)

def _layernorm(x, axis=-1, eps=1e-05):
    m = jnp.mean(x, axis=axis, keepdims=True)
    v = jnp.var(x, axis=axis, keepdims=True)
    return (x - m) / jnp.sqrt(v + eps)

def _scatter_add(tgt, idx, src, axis=0):
    return tgt.at[idx].add(src)

def _segment_sum(src, seg, n):
    return jax.ops.segment_sum(src, seg, n)
kernel_name = 'mk_macaron_d1_jaxref_r8_71fec9'

def setup_inputs(seed: int=0):
    np.random.seed(seed)
    _w = jnp.asarray

    def _L0_attn_setup():
        import jax, jax.numpy as jnp
        import numpy as np
        B, T, D, H = (8, 512, 128, 16)
        DK = D // H
        CHUNK = 64
        E, TOPK, MULT, CAPF = (8, 2, 4, 1.25)
        HID = D * MULT
        N = B * T
        CAPACITY = int(CAPF * (N / E))

        def rmsnorm(x, scale):
            return x / jnp.sqrt(jnp.mean(x * x, axis=-1, keepdims=True)) * scale

        def apply_rope(x):
            half = x.shape[-1] // 2
            t = x.shape[2]
            inv = 1.0 / 10000.0 ** (jnp.arange(half, dtype=jnp.float32) / half)
            ang = jnp.arange(t, dtype=jnp.float32)[:, None] * inv[None, :]
            sin, cos = (jnp.sin(ang)[None, None], jnp.cos(ang)[None, None])
            x1, x2 = (x[..., :half], x[..., half:])
            return jnp.concatenate([x1 * cos - x2 * sin, x1 * sin + x2 * cos], axis=-1)

        def phi(x):
            return jax.nn.elu(x) + 1.0

        def attention(x, Wq, bq, Wk, bk, Wv, bv, Wg, bg, Wo, bo):
            b, t, c = x.shape
            heads = lambda y: y.reshape(b, t, H, DK).transpose(0, 2, 1, 3)
            q = phi(apply_rope(heads(x @ Wq + bq)))
            k = phi(apply_rope(heads(x @ Wk + bk)))
            v = heads(x @ Wv + bv)
            g = heads(jax.nn.sigmoid(x @ Wg + bg))
            nc = t // CHUNK
            to_chunks = lambda y: y.reshape(b, H, nc, CHUNK, DK).transpose(2, 0, 1, 3, 4)
            qs, ks_, vs, gs = map(to_chunks, (q, k, v, g))
            S0 = jnp.zeros((b, H, DK, DK), x.dtype)
            Z0 = jnp.zeros((b, H, DK), x.dtype)

            def step(carry, inp):
                S, Z = carry
                qc, kc, vc, gc = inp
                S = S + jnp.einsum('bhtd,bhte->bhde', kc, vc)
                Z = Z + kc.sum(axis=2)
                num = jnp.einsum('bhtd,bhde->bhte', qc, S)
                den = jnp.einsum('bhtd,bhd->bht', qc, Z)[..., None] + 1e-06
                return ((S, Z), gc * (num / den))
            _, outs = jax.lax.scan(step, (S0, Z0), (qs, ks_, vs, gs))
            out = outs.transpose(1, 2, 0, 3, 4).reshape(b, H, t, DK)
            out = out.transpose(0, 2, 1, 3).reshape(b, t, c)
            return out @ Wo + bo

        def moe(x, router_W, router_b, W1, b1, W2, b2):
            b, t, c = x.shape
            n = b * t
            xf = x.reshape(n, c)
            probs = jax.nn.softmax(xf @ router_W + router_b, axis=-1)
            topk_probs, topk_idx = jax.lax.top_k(probs, TOPK)
            topk_probs = topk_probs / topk_probs.sum(axis=-1, keepdims=True)
            out = jnp.zeros_like(xf)
            load = []
            for eid in range(E):
                mask = (topk_idx == eid).reshape(-1)
                idx = jnp.nonzero(mask, size=CAPACITY, fill_value=n * TOPK)[0]
                valid = idx < n * TOPK
                idxc = jnp.minimum(idx, n * TOPK - 1)
                tok, choice = (idxc // TOPK, idxc % TOPK)
                h = jax.nn.gelu(xf[tok] @ W1[eid] + b1[eid], approximate=False) @ W2[eid] + b2[eid]
                gate = jnp.where(valid, topk_probs[tok, choice], 0.0)
                out = out.at[tok].add(gate[:, None] * h)
                load.append(jnp.minimum(mask.sum(), CAPACITY).astype(xf.dtype))
            load = jnp.stack(load)
            importance = probs.sum(axis=0)
            importance = importance / importance.sum()
            load = load / load.sum()
            aux = (importance * load).sum() * E ** 2
            return (out.reshape(b, t, c), aux)

        def _reference_tuple_inner(x, norm1_scale, norm2_scale, Wq, bq, Wk, bk, Wv, bv, Wg, bg, Wo, bo, router_W, router_b, W1, b1, W2, b2):
            x = x + attention(rmsnorm(x, norm1_scale), Wq, bq, Wk, bk, Wv, bv, Wg, bg, Wo, bo)
            moe_out, aux = moe(rmsnorm(x, norm2_scale), router_W, router_b, W1, b1, W2, b2)
            return (x + moe_out, aux)
        key = jax.random.key(seed)
        ks = jax.random.split(key, 16)
        s = 0.02
        r = lambda k, shape: jax.random.normal(k, shape, jnp.float32) * s
        return {'x': jax.random.normal(ks[0], (B, T, D), jnp.float32), 'norm1_scale': jnp.ones((D,), jnp.float32), 'norm2_scale': jnp.ones((D,), jnp.float32), 'Wq': r(ks[1], (D, D)), 'bq': jnp.zeros((D,), jnp.float32), 'Wk': r(ks[2], (D, D)), 'bk': jnp.zeros((D,), jnp.float32), 'Wv': r(ks[3], (D, D)), 'bv': jnp.zeros((D,), jnp.float32), 'Wg': r(ks[4], (D, D)), 'bg': jnp.zeros((D,), jnp.float32), 'Wo': r(ks[5], (D, D)), 'bo': jnp.zeros((D,), jnp.float32), 'router_W': r(ks[6], (D, E)), 'router_b': jnp.zeros((E,), jnp.float32), 'W1': r(ks[7], (E, D, HID)), 'b1': jnp.zeros((E, HID), jnp.float32), 'W2': r(ks[8], (E, HID, D)), 'b2': jnp.zeros((E, D), jnp.float32)}
    _L0_attn_in = _L0_attn_setup()

    def _L0_ffn_setup():
        import jax, jax.numpy as jnp
        import numpy as np
        D_MODEL = 128
        N_EXPERTS = 16
        TOP_K = 2
        EXPERT_DIM = 128
        SHARED_DIM = 256
        B, T = (2, 128)
        key = jax.random.key(seed)
        ks = jax.random.split(key, 7)
        std = 0.02
        return {'x': jax.random.normal(ks[0], (B, T, D_MODEL), dtype=jnp.float32), 'router_w': jax.random.normal(ks[1], (N_EXPERTS, D_MODEL), dtype=jnp.float32) * std, 'gate_up_w': jax.random.normal(ks[2], (N_EXPERTS, D_MODEL, 2 * EXPERT_DIM), dtype=jnp.float32) * std, 'down_w': jax.random.normal(ks[3], (N_EXPERTS, EXPERT_DIM, D_MODEL), dtype=jnp.float32) * std, 'shared_gate_w': jax.random.normal(ks[4], (SHARED_DIM, D_MODEL), dtype=jnp.float32) * std, 'shared_up_w': jax.random.normal(ks[5], (SHARED_DIM, D_MODEL), dtype=jnp.float32) * std, 'shared_down_w': jax.random.normal(ks[6], (D_MODEL, SHARED_DIM), dtype=jnp.float32) * std}
    _L0_ffn_in = _L0_ffn_setup()
    _d = {'L0_attn_x': _L0_attn_in['x'], 'L0_attn_norm1_scale': _L0_attn_in['norm1_scale'], 'L0_attn_norm2_scale': _L0_attn_in['norm2_scale'], 'L0_attn_Wq': _L0_attn_in['Wq'], 'L0_attn_bq': _L0_attn_in['bq'], 'L0_attn_Wk': _L0_attn_in['Wk'], 'L0_attn_bk': _L0_attn_in['bk'], 'L0_attn_Wv': _L0_attn_in['Wv'], 'L0_attn_bv': _L0_attn_in['bv'], 'L0_attn_Wg': _L0_attn_in['Wg'], 'L0_attn_bg': _L0_attn_in['bg'], 'L0_attn_Wo': _L0_attn_in['Wo'], 'L0_attn_bo': _L0_attn_in['bo'], 'L0_attn_router_W': _L0_attn_in['router_W'], 'L0_attn_router_b': _L0_attn_in['router_b'], 'L0_attn_W1': _L0_attn_in['W1'], 'L0_attn_b1': _L0_attn_in['b1'], 'L0_attn_W2': _L0_attn_in['W2'], 'L0_attn_b2': _L0_attn_in['b2'], 'L0_ffn_router_w': _L0_ffn_in['router_w'], 'L0_ffn_gate_up_w': _L0_ffn_in['gate_up_w'], 'L0_ffn_down_w': _L0_ffn_in['down_w'], 'L0_ffn_shared_gate_w': _L0_ffn_in['shared_gate_w'], 'L0_ffn_shared_up_w': _L0_ffn_in['shared_up_w'], 'L0_ffn_shared_down_w': _L0_ffn_in['shared_down_w']}
    _x0 = _d['L0_attn_x']
    _d['L0_attn_x'] = jax.random.normal(jax.random.fold_in(jax.random.key(seed), 1), (4, 1024, 128), dtype=_x0.dtype)
    del _x0
    return _d

def reference(L0_attn_x, L0_attn_norm1_scale, L0_attn_norm2_scale, L0_attn_Wq, L0_attn_bq, L0_attn_Wk, L0_attn_bk, L0_attn_Wv, L0_attn_bv, L0_attn_Wg, L0_attn_bg, L0_attn_Wo, L0_attn_bo, L0_attn_router_W, L0_attn_router_b, L0_attn_W1, L0_attn_b1, L0_attn_W2, L0_attn_b2, L0_ffn_router_w, L0_ffn_gate_up_w, L0_ffn_down_w, L0_ffn_shared_gate_w, L0_ffn_shared_up_w, L0_ffn_shared_down_w):

    def _L0_attn_ref(x, norm1_scale, norm2_scale, Wq, bq, Wk, bk, Wv, bv, Wg, bg, Wo, bo, router_W, router_b, W1, b1, W2, b2):
        import jax, jax.numpy as jnp
        import numpy as np
        B, T, D, H = (8, 512, 128, 16)
        DK = D // H
        CHUNK = 64
        E, TOPK, MULT, CAPF = (8, 2, 4, 1.25)
        HID = D * MULT
        N = B * T
        CAPACITY = int(CAPF * (N / E))

        def rmsnorm(x, scale):
            return x / jnp.sqrt(jnp.mean(x * x, axis=-1, keepdims=True)) * scale

        def apply_rope(x):
            half = x.shape[-1] // 2
            t = x.shape[2]
            inv = 1.0 / 10000.0 ** (jnp.arange(half, dtype=jnp.float32) / half)
            ang = jnp.arange(t, dtype=jnp.float32)[:, None] * inv[None, :]
            sin, cos = (jnp.sin(ang)[None, None], jnp.cos(ang)[None, None])
            x1, x2 = (x[..., :half], x[..., half:])
            return jnp.concatenate([x1 * cos - x2 * sin, x1 * sin + x2 * cos], axis=-1)

        def phi(x):
            return jax.nn.elu(x) + 1.0

        def attention(x, Wq, bq, Wk, bk, Wv, bv, Wg, bg, Wo, bo):
            b, t, c = x.shape
            heads = lambda y: y.reshape(b, t, H, DK).transpose(0, 2, 1, 3)
            q = phi(apply_rope(heads(x @ Wq + bq)))
            k = phi(apply_rope(heads(x @ Wk + bk)))
            v = heads(x @ Wv + bv)
            g = heads(jax.nn.sigmoid(x @ Wg + bg))
            nc = t // CHUNK
            to_chunks = lambda y: y.reshape(b, H, nc, CHUNK, DK).transpose(2, 0, 1, 3, 4)
            qs, ks_, vs, gs = map(to_chunks, (q, k, v, g))
            S0 = jnp.zeros((b, H, DK, DK), x.dtype)
            Z0 = jnp.zeros((b, H, DK), x.dtype)

            def step(carry, inp):
                S, Z = carry
                qc, kc, vc, gc = inp
                S = S + jnp.einsum('bhtd,bhte->bhde', kc, vc)
                Z = Z + kc.sum(axis=2)
                num = jnp.einsum('bhtd,bhde->bhte', qc, S)
                den = jnp.einsum('bhtd,bhd->bht', qc, Z)[..., None] + 1e-06
                return ((S, Z), gc * (num / den))
            _, outs = jax.lax.scan(step, (S0, Z0), (qs, ks_, vs, gs))
            out = outs.transpose(1, 2, 0, 3, 4).reshape(b, H, t, DK)
            out = out.transpose(0, 2, 1, 3).reshape(b, t, c)
            return out @ Wo + bo

        def moe(x, router_W, router_b, W1, b1, W2, b2):
            b, t, c = x.shape
            n = b * t
            xf = x.reshape(n, c)
            probs = jax.nn.softmax(xf @ router_W + router_b, axis=-1)
            topk_probs, topk_idx = jax.lax.top_k(probs, TOPK)
            topk_probs = topk_probs / topk_probs.sum(axis=-1, keepdims=True)
            out = jnp.zeros_like(xf)
            load = []
            for eid in range(E):
                mask = (topk_idx == eid).reshape(-1)
                idx = jnp.nonzero(mask, size=CAPACITY, fill_value=n * TOPK)[0]
                valid = idx < n * TOPK
                idxc = jnp.minimum(idx, n * TOPK - 1)
                tok, choice = (idxc // TOPK, idxc % TOPK)
                h = jax.nn.gelu(xf[tok] @ W1[eid] + b1[eid], approximate=False) @ W2[eid] + b2[eid]
                gate = jnp.where(valid, topk_probs[tok, choice], 0.0)
                out = out.at[tok].add(gate[:, None] * h)
                load.append(jnp.minimum(mask.sum(), CAPACITY).astype(xf.dtype))
            load = jnp.stack(load)
            importance = probs.sum(axis=0)
            importance = importance / importance.sum()
            load = load / load.sum()
            aux = (importance * load).sum() * E ** 2
            return (out.reshape(b, t, c), aux)

        def _reference_tuple_inner(x, norm1_scale, norm2_scale, Wq, bq, Wk, bk, Wv, bv, Wg, bg, Wo, bo, router_W, router_b, W1, b1, W2, b2):
            x = x + attention(rmsnorm(x, norm1_scale), Wq, bq, Wk, bk, Wv, bv, Wg, bg, Wo, bo)
            moe_out, aux = moe(rmsnorm(x, norm2_scale), router_W, router_b, W1, b1, W2, b2)
            return (x + moe_out, aux)
        return _reference_tuple_inner(x, norm1_scale, norm2_scale, Wq, bq, Wk, bk, Wv, bv, Wg, bg, Wo, bo, router_W, router_b, W1, b1, W2, b2)[0]

    def _L0_ffn_ref(x, router_w, gate_up_w, down_w, shared_gate_w, shared_up_w, shared_down_w):
        import jax, jax.numpy as jnp
        import numpy as np
        D_MODEL = 128
        N_EXPERTS = 16
        TOP_K = 2
        EXPERT_DIM = 128
        SHARED_DIM = 256
        B, T = (2, 128)
        Bb, Tt, C = x.shape
        N = Bb * Tt
        E = gate_up_w.shape[0]
        logits = jnp.einsum('btc,ec->bte', x, router_w)
        top_vals, top_idx = jax.lax.top_k(logits, TOP_K)
        gates = jax.nn.sigmoid(top_vals)
        xf = x.reshape(N, C)
        sel = top_idx.reshape(N, TOP_K)
        gw = gates.reshape(N, TOP_K)
        w_full = jnp.zeros((N, E), dtype=x.dtype).at[jnp.arange(N)[:, None], sel].add(gw)
        gu = jnp.einsum('nc,ech->neh', xf, gate_up_w)
        gate, up = jnp.split(gu, 2, axis=-1)
        h = jax.nn.silu(gate) * up
        out_all = jnp.einsum('neh,ehc->nec', h, down_w)
        moe = jnp.einsum('ne,nec->nc', w_full, out_all).reshape(Bb, Tt, C)
        sg = jnp.einsum('btc,sc->bts', x, shared_gate_w)
        su = jnp.einsum('btc,sc->bts', x, shared_up_w)
        shared = jnp.einsum('bts,cs->btc', jax.nn.silu(sg) * su, shared_down_w)
        return moe + shared
    x = L0_attn_x
    x = x + 0.5 * _L0_ffn_ref(_layernorm(x, axis=-1), L0_ffn_router_w, L0_ffn_gate_up_w, L0_ffn_down_w, L0_ffn_shared_gate_w, L0_ffn_shared_up_w, L0_ffn_shared_down_w)
    x = x + _L0_attn_ref(_layernorm(x, axis=-1), L0_attn_norm1_scale, L0_attn_norm2_scale, L0_attn_Wq, L0_attn_bq, L0_attn_Wk, L0_attn_bk, L0_attn_Wv, L0_attn_bv, L0_attn_Wg, L0_attn_bg, L0_attn_Wo, L0_attn_bo, L0_attn_router_W, L0_attn_router_b, L0_attn_W1, L0_attn_b1, L0_attn_W2, L0_attn_b2)
    x = x + 0.5 * _L0_ffn_ref(_layernorm(x, axis=-1), L0_ffn_router_w, L0_ffn_gate_up_w, L0_ffn_down_w, L0_ffn_shared_gate_w, L0_ffn_shared_up_w, L0_ffn_shared_down_w)
    return x

_drawn_inputs = setup_inputs


def setup_inputs(seed=0):
    import zlib

    import numpy as np

    out = dict(_drawn_inputs(seed))
    spreads = {'L0_attn_norm1_scale': (1.0, 0.6),
     'L0_attn_norm2_scale': (1.0, 0.6),
     'L0_attn_bq': (0.0, 0.8),
     'L0_attn_bk': (0.0, 0.8),
     'L0_attn_bv': (0.0, 0.8),
     'L0_attn_bg': (0.0, 0.8),
     'L0_attn_bo': (0.0, 0.1),
     'L0_attn_router_b': (0.0, 0.316),
     'L0_attn_b1': (0.0, 0.8),
     'L0_attn_b2': (0.0, 0.276)}
    factors = {'L0_attn_Wq': 8.0,
     'L0_attn_Wk': 8.0,
     'L0_attn_Wv': 8.0,
     'L0_attn_Wg': 8.0,
     'L0_attn_Wo': 7.435,
     'L0_attn_W1': 3.745,
     'L0_attn_W2': 3.403,
     'L0_ffn_router_w': 8.0,
     'L0_ffn_gate_up_w': 8.0,
     'L0_ffn_down_w': 8.0,
     'L0_ffn_shared_gate_w': 8.0,
     'L0_ffn_shared_up_w': 8.0,
     'L0_ffn_shared_down_w': 8.0}
    for name, (base, spread) in spreads.items():
        noise = np.random.default_rng([zlib.crc32(name.encode()), seed]).standard_normal(out[name].shape)
        drawn = base * np.exp(spread * noise) if base else spread * noise
        out[name] = jnp.asarray(drawn.astype(out[name].dtype))
    for name, factor in factors.items():
        out[name] = (out[name] * factor).astype(out[name].dtype)
    return out
```

```python
from contextlib import ExitStack

import numpy as np

import concourse.bass as bass
from concourse import mybir

P = 128
D = 128
BATCH = 4
SEQ_TILES = 8
TILES = BATCH * SEQ_TILES
TOKENS = TILES * P
LN_EPS = 1e-5

FFN_EXPERTS = 16
FFN_HID = 128
SHARED = 256
FFN_TILES = 80
PAIRS = FFN_TILES // 2

MOE_EXPERTS = 8
MOE_HID = 512
HID_CHUNKS = MOE_HID // P
CAPACITY = int(1.25 * (TOKENS / MOE_EXPERTS))
CAP_TILES = CAPACITY // P
MOE_TILES = MOE_EXPERTS * CAP_TILES
MOE_ROWS = MOE_TILES * P
assert CAP_TILES * P == CAPACITY
assert FFN_TILES * P >= 2 * TOKENS + FFN_EXPERTS * (P - 1) - P

HEADS = 16
DK = D // HEADS
CHUNK = 64
DEN_EPS = 1e-6

F32 = mybir.dt.float32
BF16 = mybir.dt.bfloat16
F16 = mybir.dt.float16
I32 = mybir.dt.int32
ALU = mybir.AluOpType
ACT = mybir.ActivationFunctionType
AX = mybir.AxisListType.X

CONST_WIDTHS = dict(
    ident=P, headmask=D, headcol=HEADS, before=P, ones=P, iota=P, rev=FFN_EXPERTS,
    tile_limits=TILES, restart=FFN_EXPERTS * TILES, token_id=TILES, part=1,
    expert_base=MOE_EXPERTS, cos=SEQ_TILES * DK, sin=SEQ_TILES * DK, minus_half=BATCH,
)
CONST_AT = {}
_at = 0
for _name, _width in CONST_WIDTHS.items():
    CONST_AT[_name] = (_at, _at + _width)
    _at += _width
CONST_COLS = _at
ID_SHIFT = TOKENS // 2
FAR = float(2 ** 20)


def constants():
    p = np.arange(P)
    c = {}
    c["ident"] = np.eye(P)
    c["headmask"] = (p[:, None] // DK == np.arange(D)[None] // DK)
    c["headcol"] = (p[:, None] // DK == np.arange(HEADS)[None])
    c["before"] = (p[:, None] < p[None])
    c["ones"] = np.ones((P, P))
    c["iota"] = np.tile(np.arange(P), (P, 1))
    c["rev"] = np.tile(FFN_EXPERTS - np.arange(FFN_EXPERTS), (P, 1))
    c["tile_limits"] = np.tile(P * np.arange(TILES), (P, 1))
    c["restart"] = np.tile((np.arange(FFN_EXPERTS * TILES) % TILES) != 0, (P, 1))
    c["token_id"] = P * np.arange(TILES)[None] + p[:, None] - ID_SHIFT
    c["part"] = p[:, None]
    c["expert_base"] = np.tile(CAPACITY * np.arange(MOE_EXPERTS), (P, 1))
    half = DK // 2
    inv = (1.0 / 10000.0 ** (np.arange(half, dtype=np.float32) / half)).astype(np.float32)
    angle = (np.arange(SEQ_TILES * P, dtype=np.float32)[:, None] * inv[None]).astype(np.float32)
    cos = np.cos(angle).reshape(SEQ_TILES, P, half).transpose(1, 0, 2)
    sin = np.sin(angle).reshape(SEQ_TILES, P, half).transpose(1, 0, 2)
    c["cos"] = np.concatenate([cos, cos], -1).reshape(P, -1)
    c["sin"] = np.concatenate([sin, -sin], -1).reshape(P, -1)
    c["minus_half"] = np.full((P, BATCH), -0.5)
    return np.concatenate([c[n].astype(np.float32) for n in CONST_WIDTHS], axis=1)


class Core:
    pass


class Linked:

    def __init__(self, eng, done):
        self.eng, self.done, self.n = eng, done, 0

    def __call__(self, ins):
        self.n += 1
        ins.then_inc(self.done, 1)
        self.eng.wait_ge(self.done, self.n)


class Scope:

    def __init__(self, nc, tag):
        self.nc, self.tag, self.stack = nc, tag, ExitStack()

    def __enter__(self):
        return self

    def __exit__(self, *a):
        self.stack.close()

    def sb(self, name, shape, dt=F32):
        return self.stack.enter_context(self.nc.sbuf_tensor(f"{self.tag}_{name}", shape, dt))

    def ps(self, name, shape=(P, 512), dt=F32):
        return self.stack.enter_context(self.nc.psum_tensor(f"{self.tag}_{name}", list(shape), dt))

    def sem(self, name):
        return self.stack.enter_context(self.nc.semaphore(f"{self.tag}_{name}"))


def spread(ap, n, inner=True):
    m = ap.shape[1]
    return ap.unsqueeze(2).to_broadcast([P, m, n]) if inner else ap.unsqueeze(1).to_broadcast([P, n, m])



def load_all(nc, core, w, x):
    with Scope(nc, "init") as s, nc.Block() as block:
        x_steps = x.rearrange("b (j p) d -> j p b d", p=P)
        late = [
            (core.gate_up[:], w["gate_up"].rearrange("e c h -> c e h")),
            (core.down[:], w["down"].rearrange("e h c -> h e c")),
        ]
        early = [
            (core.const[:], w["const"]),
            (core.ffn_router[:], w["ffn_router"]),
            (core.shared_gate[:], w["shared_gate"]),
            (core.shared_up[:], w["shared_up"]),
            (core.shared_down[:], w["shared_down"].rearrange("(h s) c -> s h c", s=P)),
            (core.qkvg[:, 0, :], w["wq"]), (core.qkvg[:, 1, :], w["wk"]),
            (core.qkvg[:, 2, :], w["wv"]), (core.qkvg[:, 3, :], w["wg"]),
            (core.wo[:], w["wo"]),
            (core.norm1[:], w["norm1"].rearrange("(c a) -> c a", a=1)),
            (core.norm2[:], w["norm2"].rearrange("(c a) -> c a", a=1)),
            (core.moe_router[:], w["moe_router"]),
            (core.router_bias[:], w["router_bias"].rearrange("(a e) -> a e", a=1).to_broadcast([P, MOE_EXPERTS])),
            (core.b1[:], w["b1"]),
        ]
        loaded = s.sem("loaded")
        rows = [("bq", 0), ("bk", D), ("bv", 2 * D), ("bg", 3 * D), ("bo", 4 * D)]
        row = s.sb("row", [1, core.bias_cols])
        rest = s.sb("rest", [1, core.bias_cols])
        parts = s.sb("parts", [1, 3, core.bias_cols], BF16)
        row_loaded, split, step = s.sem("row_loaded"), s.sem("split"), s.sem("step")
        zero = s.sb("zero", [P, D])
        zeroed, zero_stored = s.sem("zeroed"), s.sem("zero_stored")

        @block.sync
        def _(sp):
            for j in range(SEQ_TILES):
                sp.dma_start(core.x[:, :, j, :], x_steps[j]).then_inc(loaded, 16)
            for dst, src in early:
                sp.dma_start(dst, src).then_inc(loaded, 16)
            sp.wait_ge(loaded, 16 * (SEQ_TILES + len(early)))

        @block.scalar
        def _(act):
            for name, at in rows:
                act.dma_start(row[:, at:at + D], w[name].rearrange("(a n) -> a n", a=1)).then_inc(row_loaded, 16)
            act.dma_start(row[:, 5 * D:], w["b2"].rearrange("(a e) n -> a (e n)", a=1)).then_inc(row_loaded, 16)
            for dst, src in late:
                act.dma_start(dst, src).then_inc(row_loaded, 16)
            for e in range(MOE_EXPERTS):
                act.dma_start(core.w1[:, e, :], w["w1"][e]).then_inc(row_loaded, 16)
                act.dma_start(core.w2[:, e, :, :], w["w2"][e].rearrange("(k p) c -> p k c", p=P)).then_inc(row_loaded, 16)
            act.wait_ge(split, 1)
            for k in range(3):
                act.dma_start(core.bias3[k:k + 1, :], parts[:, k, :]).then_inc(row_loaded, 16)
            act.wait_ge(zeroed, 1)
            act.dma_start(core.moe_out_rows[MOE_ROWS:MOE_ROWS + P, :], zero[:]).then_inc(zero_stored, 16)
            act.wait_ge(zero_stored, 16)
            act.wait_ge(row_loaded, 16 * (len(rows) + 1 + len(late) + 2 * MOE_EXPERTS + 3))

        @block.vector
        def _(vec):
            link = Linked(vec, step)
            nc.vector.memset(zero[:], 0.0).then_inc(zeroed, 1)
            vec.wait_ge(row_loaded, 16 * (len(rows) + 1 + len(late) + 2 * MOE_EXPERTS))
            link(nc.vector.tensor_copy(parts[:, 0, :], row[:]))
            link(nc.vector.tensor_tensor(rest[:], row[:], parts[:, 0, :], ALU.subtract))
            link(nc.vector.tensor_copy(parts[:, 1, :], rest[:]))
            link(nc.vector.tensor_tensor(row[:], rest[:], parts[:, 1, :], ALU.subtract))
            nc.vector.tensor_copy(parts[:, 2, :], row[:]).then_inc(split, 1)
            vec.wait_ge(loaded, 16 * (SEQ_TILES + len(early)))
            nc.vector.tensor_copy(core.before16[:], core.c("before"))
            nc.vector.tensor_copy(core.ones16[:], core.c("ones"))
            nc.vector.tensor_copy(core.iota16[:], core.c("iota"))
            nc.vector.tensor_copy(core.ones_bf[:], core.c("ones")[0:3, :])



def statistics(nc, link, vec, x, stats, mean_var, ready):
    for b in range(BATCH):
        last = nc.vector.bn_stats(stats[:, b, :], x[:, b, :])
    link(last)
    for b in range(BATCH):
        last = nc.vector.bn_aggr(mean_var[:, b, :], stats[:, b, :])
    last.then_inc(ready, 1)


def top_two(nc, link, values, rev, one_hots, tops, scratch):
    n, e = values.shape[1], values.shape[2]
    same, first = scratch
    rank = spread(rev, n, inner=False)
    for k in range(2):
        link(nc.vector.tensor_reduce(tops[k], values, axis=AX, op=ALU.max))
        link(nc.vector.tensor_tensor(same, values, spread(tops[k], e), ALU.is_equal))
        link(nc.vector.tensor_tensor(same, same, rank, ALU.mult))
        link(nc.vector.tensor_reduce(first, same, axis=AX, op=ALU.max))
        link(nc.vector.tensor_tensor(one_hots[k], rank, spread(first, e), ALU.is_equal))
        if k == 0:
            link(nc.vector.scalar_tensor_tensor(values, one_hots[0], -1e30, values, ALU.mult, ALU.add))


class Returned:

    def __init__(self, s, rows, back_slot, gates):
        self.rows, self.back_slot, self.gates = rows, back_slot, gates
        self.got = [s.sb(f"back{k}", [P, 2, BATCH, D]) for k in range(2)]
        self.arrived = [s.sem(f"back_arrived{k}") for k in range(2)]
        self.used, self.half = s.sem("back_used"), s.sem("back_half")

    def gather(self, pool, j):
        if j >= 2:
            pool.wait_ge(self.used, j - 1)
        for k in range(2):
            for b in range(BATCH):
                t = SEQ_TILES * b + j
                pool.indirect_dma_start(
                    out=self.got[j % 2][:, k, b, :], out_offset=None, in_=self.rows,
                    in_offset=bass.IndirectOffsetOnAxis(ap=self.back_slot[:, k, t:t + 1], axis=0),
                ).then_inc(self.arrived[j % 2], 16)

    def add(self, nc, vec, x, j):
        vec.wait_ge(self.arrived[j % 2], 16 * 2 * BATCH * (j // 2 + 1))
        for k, done in enumerate((self.half, self.used)):
            for b in range(BATCH):
                t = SEQ_TILES * b + j
                last = nc.vector.scalar_tensor_tensor(
                    x[:, b, :], self.got[j % 2][:, k, b, :], self.gates[:, k, t:t + 1], x[:, b, :], ALU.mult, ALU.add)
            last.then_inc(done, 1)
            vec.wait_ge(done, j + 1)



def ffn_front(nc, core, tag, combine=None):
    with Scope(nc, tag) as s, nc.Block() as block:
        norm = [s.sb(f"norm{k}", [P, BATCH, D]) for k in range(2)]
        norm_t = [s.sb(f"norm_t{k}", [P, BATCH * P]) for k in range(2)]
        gate = s.sb("gate", [P, 2, BATCH * P])
        hid = [s.sb(f"hid{k}", [P, 2, BATCH * P]) for k in range(2)]
        stats = s.sb("stats", [P, BATCH, 6])
        mean_var = [s.sb(f"mean_var{k}", [P, BATCH, 2]) for k in range(2)]
        var_eps = s.sb("var_eps", [P, BATCH])
        rstd = [s.sb(f"rstd{k}", [P, BATCH]) for k in range(2)]
        logits = s.sb("logits", [P, BATCH, FFN_EXPERTS])
        same = s.sb("same", [P, BATCH, FFN_EXPERTS])
        first = s.sb("first", [P, BATCH])
        t_ps = [s.ps(f"t{k}") for k in range(2)]
        logits_ps, down_ps = s.ps("logits_ps"), s.ps("down_ps")
        gate_ps = [s.ps(f"gate_ps{k}") for k in range(2)]
        up_ps = [s.ps(f"up_ps{k}") for k in range(2)]

        stats_ready, rstd_ready, pool_step, vec_step = (s.sem(n) for n in ("stats_ready", "rstd_ready", "pool_step", "vec_step"))
        norm_ready, turned, turn_copied, logits_done, logits_read = (
            s.sem(n) for n in ("norm_ready", "turned", "turn_copied", "logits_done", "logits_read"))
        gate_done, up_done, silu_done, hid_ready, down_done, x_updated = (
            s.sem(n) for n in ("gate_done", "up_done", "silu_done", "hid_ready", "down_done", "x_updated"))
        stored = [s.sem(f"stored{k}") for k in range(2)]
        back = Returned(s, *combine) if combine else None
        rows = core.norm_rows.rearrange("(b j p) d -> j p b d", p=P, j=SEQ_TILES)

        @block.sync
        def _(sp):
            for j in range(SEQ_TILES):
                sp.wait_ge(norm_ready, j + 1)
                sp.dma_start(rows[j], norm[j % 2][:]).then_inc(stored[j % 2], 16)
            for k in range(2):
                sp.wait_ge(stored[k], 16 * (SEQ_TILES // 2))

        @block.gpsimd
        def _(pool):
            link = Linked(pool, pool_step)
            if back:
                back.gather(pool, 0)
            for j in range(SEQ_TILES):
                if back and j + 1 < SEQ_TILES:
                    back.gather(pool, j + 1)
                pool.wait_ge(stats_ready, j + 1)
                link(pool.tensor_scalar(var_eps[:], mean_var[j % 2][:, :, 1], LN_EPS, None, ALU.add))
                if j >= 2:
                    pool.wait_ge(norm_ready, j - 1)
                pool.tensor_tensor(rstd[j % 2][:], var_eps[:], core.c("minus_half"), ALU.pow).then_inc(rstd_ready, 1)

        @block.scalar
        def _(act):
            for j in range(SEQ_TILES):
                act.wait_ge(turned, j + 1)
                if j >= 2:
                    act.wait_ge(up_done, 2 * (j - 1))
                nc.scalar.activation(norm_t[j % 2][:], t_ps[j % 2][:], ACT.Copy).then_inc(turn_copied, 1)
                for h in range(2):
                    act.wait_ge(gate_done, 2 * j + h + 1)
                    if h == 0 and j >= 1:
                        act.wait_ge(hid_ready, j)
                    nc.scalar.activation(gate[:, h, :], gate_ps[h][:], ACT.Silu).then_inc(silu_done, 1)

        @block.vector
        def _(vec):
            link = Linked(vec, vec_step)
            for i in range(-1, SEQ_TILES + 1):
                j = i + 1
                if j < SEQ_TILES:
                    xj = core.x[:, :, j, :]
                    if back:
                        back.add(nc, vec, xj, j)
                    statistics(nc, link, vec, xj, stats, mean_var[j % 2], stats_ready)
                if i >= 1:
                    vec.wait_ge(down_done, i)
                    xi = core.x[:, :, i - 1, :]
                    nc.vector.scalar_tensor_tensor(
                        xi, down_ps[:].rearrange("p (b d) -> p b d", d=D), 0.5, xi, ALU.mult, ALU.add
                    ).then_inc(x_updated, 1)
                if 0 <= i < SEQ_TILES:
                    vec.wait_ge(logits_done, i + 1)
                    nc.vector.tensor_copy(
                        logits[:].rearrange("p b e -> p (b e)"), logits_ps[:, 0:BATCH * FFN_EXPERTS]
                    ).then_inc(logits_read, 1)
                if j < SEQ_TILES:
                    vec.wait_ge(rstd_ready, j + 1)
                    if j >= 2:
                        vec.wait_ge(turned, j - 1)
                        vec.wait_ge(stored[j % 2], 16 * (j // 2))
                    for b in range(BATCH):
                        last = nc.vector.tensor_scalar(
                            norm[j % 2][:, b, :], xj[:, b, :], mean_var[j % 2][:, b, 0:1],
                            rstd[j % 2][:, b:b + 1], ALU.subtract, ALU.mult)
                    last.then_inc(norm_ready, 1)
                if 0 <= i < SEQ_TILES:
                    for h in range(2):
                        vec.wait_ge(silu_done, 2 * i + h + 1)
                        vec.wait_ge(up_done, 2 * i + h + 1)
                        if h == 0 and i >= 2:
                            vec.wait_ge(down_done, i - 1)
                        last = nc.vector.tensor_tensor(hid[i % 2][:, h, :], gate[:, h, :], up_ps[h][:], ALU.mult)
                    last.then_inc(hid_ready, 1)
                    here = slice(i, TILES, SEQ_TILES)
                    vec.wait_ge(logits_read, i + 1)
                    top_two(nc, link, logits[:], core.c("rev"),
                            [core.pick[k][:, here, :] for k in range(2)],
                            [core.tops[:, k, here] for k in range(2)], (same[:], first[:]))

        @block.tensor
        def _(pe):
            for i in range(SEQ_TILES + 1):
                if i < SEQ_TILES:
                    pe.wait_ge(norm_ready, i + 1)
                    if i >= 2:
                        pe.wait_ge(turn_copied, i - 1)
                    for b in range(BATCH):
                        last = nc.tensor.transpose(t_ps[i % 2][:, b * P:(b + 1) * P], norm[i % 2][:, b, :], core.c("ident"))
                    last.then_inc(turned, 1)
                if i >= 1:
                    pe.wait_ge(hid_ready, i)
                    if i >= 2:
                        pe.wait_ge(x_updated, i - 1)
                    for b in range(BATCH):
                        for h in range(2):
                            last = nc.tensor.matmul(
                                down_ps[:, b * D:(b + 1) * D], hid[(i - 1) % 2][:, h, b * P:(b + 1) * P],
                                core.shared_down[:, h, :], start=(h == 0), stop=(h == 1))
                    last.then_inc(down_done, 1)
                if i < SEQ_TILES:
                    pe.wait_ge(turn_copied, i + 1)
                    if i >= 1:
                        pe.wait_ge(logits_read, i)
                    for b in range(BATCH):
                        last = nc.tensor.matmul(
                            logits_ps[:, b * FFN_EXPERTS:(b + 1) * FFN_EXPERTS], norm_t[i % 2][:, b * P:(b + 1) * P],
                            core.ffn_router[:], start=True, stop=True)
                    last.then_inc(logits_done, 1)
                    for h in range(2):
                        if i >= 1:
                            pe.wait_ge(silu_done, 2 * (i - 1) + h + 1)
                        nc.tensor.matmul(gate_ps[h][:], core.shared_gate[:, h * P:(h + 1) * P], norm_t[i % 2][:],
                                         start=True, stop=True).then_inc(gate_done, 1)
                        nc.tensor.matmul(up_ps[h][:], core.shared_up[:, h * P:(h + 1) * P], norm_t[i % 2][:],
                                         start=True, stop=True).then_inc(up_done, 1)



def rank(nc, core, tag, pick, experts, tiles, capacity=None):
    cells = experts * TILES
    choices = 2 * TILES
    per_group = 8
    groups = choices // per_group
    with Scope(nc, tag) as s, nc.Block() as block:
        both = s.sb("both", [P, experts, TILES], F16)
        upto = s.sb("upto", [P, experts, TILES])
        place = s.sb("place", [P, experts, TILES])
        work = s.sb("work", [P, experts, TILES])
        used_tiles, ends, base = (s.sb(n, [P, experts]) for n in ("used_tiles", "ends", "base"))
        picked = s.sb("picked", [P, TILES, experts])
        slot = s.sb("slot", [P, 2, TILES])
        slot_int, hi_int, lo_int = (s.sb(n, [P, choices], I32) for n in ("slot_int", "hi_int", "lo_int"))
        clamped = s.sb("clamped", [P, 2, TILES])
        hi, lo = s.sb("hi", [P, choices]), s.sb("lo", [P, choices])
        lo_hot = [s.sb(f"lo_hot{k}", [P, per_group, P], F16) for k in range(2)]
        hi_hot = [s.sb(f"hi_hot{k}", [P, per_group, tiles], F16) for k in range(2)]
        whose = s.sb("whose", [P, 1])
        tanh = s.sb("tanh", [P, 2, TILES])
        before_ps, total_ps, token_ps, whose_ps = (s.ps(n) for n in ("before_ps", "total_ps", "token_ps", "whose_ps"))
        both_ready, counted, vec_step, hot_ready, hot_used, tokens_done = (
            s.sem(n) for n in ("both_ready", "counted", "vec_step", "hot_ready", "hot_used", "tokens_done"))
        whose_ready, whose_turned, tanh_done = (s.sem(n) for n in ("whose_ready", "whose_turned", "tanh_done"))
        by_expert = lambda ap: ap.rearrange("p t e -> p e t")
        flat = lambda ap: ap.rearrange("p e t -> p (e t)")

        @block.scalar
        def _(act):
            if capacity is None:
                nc.scalar.activation(tanh[:], core.tops[:], ACT.Tanh, scale=0.5).then_inc(tanh_done, 1)

        @block.vector
        def _(vec):
            link = Linked(vec, vec_step)
            nc.vector.tensor_tensor(both[:], by_expert(pick[0]), by_expert(pick[1]), ALU.add).then_inc(both_ready, 1)
            if capacity is None:
                vec.wait_ge(tanh_done, 1)
                nc.vector.tensor_scalar(core.gates[:], tanh[:], 0.25, 0.25, ALU.mult, ALU.add)
            vec.wait_ge(counted, 1)
            link(nc.vector.tensor_tensor_scan(
                flat(upto[:]), core.c("restart")[:, 0:cells], total_ps[:, 0:cells], 0.0, ALU.mult, ALU.add))
            link(nc.vector.tensor_tensor(flat(work[:]), flat(upto[:]), total_ps[:, 0:cells], ALU.subtract))
            link(nc.vector.tensor_tensor(flat(place[:]), flat(work[:]), before_ps[:, 0:cells], ALU.add))
            if capacity is None:
                link(nc.vector.tensor_tensor(
                    work[:], spread(upto[:, :, TILES - 1], TILES), spread(core.c("tile_limits"), experts, inner=False), ALU.is_gt))
                link(nc.vector.tensor_reduce(used_tiles[:], work[:], axis=AX, op=ALU.add))
                link(nc.vector.tensor_tensor_scan(ends[:], core.c("ones")[:, 0:experts], used_tiles[:], 0.0, ALU.mult, ALU.add))
                link(nc.vector.tensor_tensor(base[:], ends[:], used_tiles[:], ALU.subtract))
                link(nc.vector.scalar_tensor_tensor(place[:], spread(base[:], TILES), float(P), place[:], ALU.mult, ALU.add))
                nc.vector.tensor_scalar(base[0:tiles, :], ends[0:tiles, :], core.c("part")[0:tiles, :], None,
                                        ALU.is_le, ALU.add, accum_out=whose[0:tiles, :]).then_inc(whose_ready, 1)
            else:
                link(nc.vector.tensor_scalar(work[:], place[:], float(capacity), FAR, ALU.is_ge, ALU.mult))
                link(nc.vector.tensor_tensor(place[:], place[:], work[:], ALU.add))
                link(nc.vector.tensor_tensor(place[:], place[:], spread(core.c("expert_base"), TILES), ALU.add))
            for k in range(2):
                link(nc.vector.tensor_tensor(picked[:], pick[k], place[:].rearrange("p e t -> p t e"), ALU.mult))
                link(nc.vector.tensor_reduce(slot[:, k, :], picked[:], axis=AX, op=ALU.add))
            slots = slot[:].rearrange("p k t -> p (k t)")
            link(nc.vector.tensor_copy(slot_int[:], slots))
            link(nc.vector.tensor_single_scalar(hi_int[:], slot_int[:], 7, ALU.arith_shift_right))
            link(nc.vector.tensor_single_scalar(lo_int[:], slot_int[:], P - 1, ALU.bitwise_and))
            link(nc.vector.tensor_copy(hi[:], hi_int[:]))
            link(nc.vector.tensor_copy(lo[:], lo_int[:]))
            for g in range(groups):
                if g >= 2:
                    vec.wait_ge(hot_used, g - 1)
                for u in range(per_group):
                    n = g * per_group + u
                    nc.vector.tensor_scalar(lo_hot[g % 2][:, u, :], core.iota16[:], lo[:, n:n + 1], None, ALU.is_equal)
                    last = nc.vector.tensor_scalar(
                        hi_hot[g % 2][:, u, :], core.iota16[:, 0:tiles], hi[:, n:n + 1],
                        core.c("token_id")[:, n % TILES:n % TILES + 1], ALU.is_equal, ALU.mult)
                last.then_inc(hot_ready, 1)
            if capacity is None:
                nc.vector.tensor_copy(core.back_slot[:], slot[:])
                vec.wait_ge(whose_turned, 1)
                nc.vector.tensor_scalar(core.expert_ids[:], whose_ps[0:1, 0:tiles], float(experts - 1), None, ALU.min)
            else:
                link(nc.vector.tensor_scalar(clamped[:], slot[:], float(experts * capacity), None, ALU.min))
                nc.vector.tensor_copy(core.back_slot[:], clamped[:])
            vec.wait_ge(tokens_done, 1)
            nc.vector.tensor_scalar(core.gather_id[:, 0:tiles], token_ps[:, 0:tiles], float(ID_SHIFT), None, ALU.add)

        @block.tensor
        def _(pe):
            pe.wait_ge(both_ready, 1)
            nc.tensor.matmul(before_ps[:, 0:cells], core.before16[:], flat(both[:]), start=True, stop=True)
            nc.tensor.matmul(total_ps[:, 0:cells], core.ones16[:], flat(both[:]), start=True, stop=True).then_inc(counted, 1)
            if capacity is None:
                pe.wait_ge(whose_ready, 1)
                nc.tensor.matmul(whose_ps[0:1, 0:tiles], whose[0:tiles, :], core.c("ident")[0:tiles, 0:tiles],
                                 start=True, stop=True).then_inc(whose_turned, 1)
            for g in range(groups):
                pe.wait_ge(hot_ready, g + 1)
                for u in range(per_group):
                    n = g * per_group + u
                    last = nc.tensor.matmul(token_ps[:, 0:tiles], lo_hot[g % 2][:, u, :], hi_hot[g % 2][:, u, :],
                                            start=(n == 0), stop=(n == choices - 1))
                last.then_inc(tokens_done if g == groups - 1 else hot_used, 1)



def ffn_experts(nc, core, tag):
    ring = 4
    with Scope(nc, tag) as s, nc.Block() as block:
        rows = [s.sb(f"rows{k}", [P, 2, D]) for k in range(ring)]
        rows_t = [s.sb(f"rows_t{k}", [P, 2 * P]) for k in range(2)]
        gate = [s.sb(f"gate{k}", [P, 2, FFN_HID]) for k in range(2)]
        hid = [s.sb(f"hid{k}", [P, 2, FFN_HID]) for k in range(2)]
        hid_t = [s.sb(f"hid_t{k}", [P, 2 * P]) for k in range(2)]
        out = [s.sb(f"out{k}", [P, 2, D]) for k in range(2)]
        t_ps = [s.ps(f"t_ps{k}") for k in range(2)]
        gu_ps = [s.ps(f"gu_ps{k}", [P, 2, 2 * FFN_HID]) for k in range(2)]
        ht_ps = [s.ps(f"ht_ps{k}") for k in range(2)]
        out_ps = [s.ps(f"out_ps{k}") for k in range(2)]
        arrived = [s.sem(f"arrived{k}") for k in range(ring)]
        stored = [s.sem(f"stored{k}") for k in range(2)]
        turned, turn_copied, gu_done, silu_done, hid_ready = (
            s.sem(n) for n in ("turned", "turn_copied", "gu_done", "silu_done", "hid_ready"))
        hid_turned, hid_copied, out_done, out_copied = (
            s.sem(n) for n in ("hid_turned", "hid_copied", "out_done", "out_copied"))
        stores = core.ffn_out_rows.rearrange("(a p) d -> p a d", p=P)


        @block.gpsimd
        def _(pool):
            for i in range(PAIRS):
                if i >= ring:
                    pool.wait_ge(turned, i - ring + 1)
                for h in range(2):
                    tile = 2 * i + h
                    pool.indirect_dma_start(
                        out=rows[i % ring][:, h, :], out_offset=None, in_=core.norm_rows,
                        in_offset=bass.IndirectOffsetOnAxis(ap=core.gather_id[:, tile:tile + 1], axis=0),
                    ).then_inc(arrived[i % ring], 16)

        @block.tensor
        def _(pe):
            expert = {}
            for i in range(PAIRS + 3):
                if i < PAIRS:
                    pe.wait_ge(arrived[i % ring], 32 * (i // ring + 1))
                    for h in range(2):
                        last = nc.tensor.transpose(t_ps[i % 2][:, h * P:(h + 1) * P], rows[i % ring][:, h, :], core.c("ident"))
                    last.then_inc(turned, 1)
                q = i - 1
                if 0 <= q < PAIRS:
                    for h in range(2):
                        expert[2 * q + h] = pe.value_load(
                            core.expert_ids[0:1, 2 * q + h:2 * q + h + 1], min_val=0, max_val=FFN_EXPERTS - 1)
                    pe.wait_ge(turn_copied, q + 1)
                    for h in range(2):
                        last = nc.tensor.matmul(gu_ps[q % 2][:, h, :], rows_t[q % 2][:, h * P:(h + 1) * P],
                                                core.gate_up[:, expert[2 * q + h], :], start=True, stop=True)
                    last.then_inc(gu_done, 1)
                q = i - 2
                if 0 <= q < PAIRS:
                    pe.wait_ge(hid_ready, q + 1)
                    for h in range(2):
                        last = nc.tensor.transpose(ht_ps[q % 2][:, h * P:(h + 1) * P], hid[q % 2][:, h, :], core.c("ident"))
                    last.then_inc(hid_turned, 1)
                q = i - 3
                if 0 <= q < PAIRS:
                    pe.wait_ge(hid_copied, q + 1)
                    if q >= 2:
                        pe.wait_ge(out_copied, q - 1)
                    for h in range(2):
                        last = nc.tensor.matmul(out_ps[q % 2][:, h * P:(h + 1) * P], hid_t[q % 2][:, h * P:(h + 1) * P],
                                                core.down[:, expert.pop(2 * q + h), :], start=True, stop=True)
                    last.then_inc(out_done, 1)

        @block.scalar
        def _(act):
            for i in range(PAIRS + 3):
                if i < PAIRS:
                    act.wait_ge(turned, i + 1)
                    if i >= 2:
                        act.wait_ge(gu_done, i - 1)
                    nc.scalar.activation(rows_t[i % 2][:], t_ps[i % 2][:, 0:2 * P], ACT.Copy).then_inc(turn_copied, 1)
                q = i - 1
                if 0 <= q < PAIRS:
                    act.wait_ge(gu_done, q + 1)
                    if q >= 2:
                        act.wait_ge(hid_ready, q - 1)
                    nc.scalar.activation(gate[q % 2][:], gu_ps[q % 2][:, :, 0:FFN_HID], ACT.Silu).then_inc(silu_done, 1)
                q = i - 3
                if 0 <= q < PAIRS:
                    act.wait_ge(out_done, q + 1)
                    if q >= 2:
                        act.wait_ge(stored[q % 2], 16 * (q // 2))
                    nc.scalar.activation(out[q % 2][:], out_ps[q % 2][:, 0:2 * P].rearrange("p (h d) -> p h d", d=D),
                                         ACT.Copy).then_inc(out_copied, 1)

        @block.vector
        def _(vec):
            for i in range(PAIRS + 2):
                q = i - 1
                if 0 <= q < PAIRS:
                    vec.wait_ge(silu_done, q + 1)
                    if q >= 2:
                        vec.wait_ge(hid_turned, q - 1)
                    nc.vector.tensor_tensor(hid[q % 2][:], gate[q % 2][:], gu_ps[q % 2][:, :, FFN_HID:], ALU.mult).then_inc(hid_ready, 1)
                q = i - 2
                if 0 <= q < PAIRS:
                    vec.wait_ge(hid_turned, q + 1)
                    if q >= 2:
                        vec.wait_ge(out_done, q - 1)
                    nc.vector.tensor_copy(hid_t[q % 2][:], ht_ps[q % 2][:, 0:2 * P]).then_inc(hid_copied, 1)

        @block.sync
        def _(sp):
            for q in range(PAIRS):
                sp.wait_ge(out_copied, q + 1)
                sp.dma_start(stores[:, 2 * q:2 * q + 2, :], out[q % 2][:]).then_inc(stored[q % 2], 16)
            for k in range(2):
                sp.wait_ge(stored[k], 16 * (PAIRS // 2))



class Ring:

    def __init__(self, s, name, plan):
        self.banks = [s.ps(f"{name}{k}") for k in range(2)]
        self.filled = [s.sem(f"{name}_filled{k}") for k in range(2)]
        self.emptied = [s.sem(f"{name}_emptied{k}") for k in range(2)]
        self.at = {use: divmod(n, 2) for n, use in enumerate(plan)}

    def bank(self, *use):
        return self.banks[self.at[use][1]]

    def claim(self, pe, *use):
        turn, k = self.at[use]
        if turn:
            pe.wait_ge(self.emptied[k], turn)

    def fill(self, ins, *use):
        ins.then_inc(self.filled[self.at[use][1]], 1)

    def await_filled(self, eng, *use):
        turn, k = self.at[use]
        eng.wait_ge(self.filled[k], turn + 1)

    def empty(self, ins, *use):
        ins.then_inc(self.emptied[self.at[use][1]], 1)

    def await_emptied(self, eng, *use):
        turn, k = self.at[use]
        eng.wait_ge(self.emptied[k], turn + 1)


def attention(nc, core, tag, combine):
    S = SEQ_TILES
    first, end = -2, S + 4
    zcols = D + HEADS
    within = lambda j: 0 <= j < S

    def plan():
        for i in range(first, end):
            for what, j in (("out_t", i - 2), ("r1_t", i + 1), ("wo", i - 2), ("r2_t", i - 3), ("q_t", i - 1), ("logits", i - 3)):
                if within(j):
                    yield what, j

    with Scope(nc, tag) as s, nc.Block() as block:
        back = Returned(s, *combine)
        stats = s.sb("stats", [P, BATCH, 6])
        mean_var = [s.sb(f"mean_var{k}", [P, BATCH, 2]) for k in range(2)]
        var_eps, ms, ms2 = (s.sb(n, [P, BATCH]) for n in ("var_eps", "ms", "ms2"))
        rstd = [s.sb(f"rstd{k}", [P, BATCH]) for k in range(2)]
        rms1 = [s.sb(f"rms1{k}", [P, BATCH]) for k in range(2)]
        rms2 = s.sb("rms2", [P, BATCH])
        sum_sq = s.sb("sum_sq", [P, BATCH])
        norm = [s.sb(f"norm{k}", [P, BATCH, D]) for k in range(4)]
        r1 = [s.sb(f"r1_{k}", [P, BATCH, D]) for k in range(2)]
        r1_t = [s.sb(f"r1_t{k}", [P, BATCH * P]) for k in range(2)]
        turned_qk = s.sb("turned_qk", [P, BATCH, 2 * D])
        sin_part = s.sb("sin_part", [P, BATCH, 2 * D])
        exp_qk = s.sb("exp_qk", [P, BATCH, 2 * D])
        relu_qk = s.sb("relu_qk", [P, BATCH, 2 * D])
        phi = [s.sb(f"phi{k}", [P, BATCH, 2 * D]) for k in range(2)]
        v1 = [s.sb(f"v1_{k}", [P, BATCH, D + 1]) for k in range(2)]
        tanh = [s.sb(f"tanh{k}", [P, BATCH, D]) for k in range(2)]
        q_t = s.sb("q_t", [P, BATCH * P])
        state = [s.sb(f"state{c}", [P, BATCH, zcols]) for c in range(2)]
        den, recip = s.sb("den", [P, BATCH, HEADS]), s.sb("recip", [P, BATCH, HEADS])
        gated = s.sb("gated", [P, BATCH, D])
        heads = s.sb("heads", [P, BATCH, D])
        heads_t = s.sb("heads_t", [P, BATCH * P])
        a1 = s.sb("a1", [P, BATCH, D])
        square = s.sb("square", [P, BATCH, D])
        r2 = [s.sb(f"r2_{k}", [P, BATCH, D]) for k in range(2)]
        r2_t = s.sb("r2_t", [P, BATCH * P])

        ring = Ring(s, "ring", plan())
        qk_ps, vg_ps = s.ps("qk_ps"), s.ps("vg_ps")
        kv_ps = s.ps("kv_ps", [P, 2, 512])
        num_ps = s.ps("num_ps", [P, 2, 512])

        names = ("stats_ready", "rstd_ready", "rms1_ready", "rms2_ready", "pool_step", "vec_step", "norm_ready",
                 "qk_done", "qk_read", "vg_done", "vg_read", "rope_ready", "act_done", "phi_ready",
                 "kv_done", "state_ready", "num_done", "num_read", "heads_ready", "a1_ready", "sums_ready", "r2_ready",
                 "v_ones")
        sig = {n: s.sem(n) for n in names}
        r2_stored = [s.sem(f"r2_stored{k}") for k in range(2)]
        rows = core.moe_rows.rearrange("(b j p) d -> j p b d", p=P, j=S)
        four = lambda ap: ap.rearrange("p (a c) n -> p a c n", c=2)
        kv = kv_ps[:, :, 0:2 * (D + 1)].rearrange("p a (c n) -> p a c n", n=D + 1)
        num = num_ps[:, :, 0:2 * zcols].rearrange("p a (c n) -> p a c n", n=zcols)

        @block.sync
        def _(sp):
            for j in range(S):
                sp.wait_ge(sig["r2_ready"], j + 1)
                sp.dma_start(rows[j], r2[j % 2][:]).then_inc(r2_stored[j % 2], 16)
            for k in range(2):
                sp.wait_ge(r2_stored[k], 16 * (S // 2))

        @block.gpsimd
        def _(pool):
            link = Linked(pool, sig["pool_step"])
            half = core.c("minus_half")
            back.gather(pool, 0)
            for i in range(first, end):
                if within(i + 3):
                    back.gather(pool, i + 3)
                j = i + 2
                if within(j):
                    pool.wait_ge(sig["stats_ready"], j + 1)
                    var = mean_var[j % 2][:, :, 1]
                    link(pool.tensor_scalar(var_eps[:], var, LN_EPS, None, ALU.add))
                    if j >= 2:
                        pool.wait_ge(sig["norm_ready"], j - 1)
                    link(pool.tensor_tensor(rstd[j % 2][:], var_eps[:], half, ALU.pow))
                    link(pool.tensor_tensor(ms[:], rstd[j % 2][:], rstd[j % 2][:], ALU.mult))
                    link(pool.tensor_tensor(ms[:], ms[:], var, ALU.mult))
                    link(pool.tensor_tensor(ms2[:], ms[:], half, ALU.pow))
                    pool.tensor_tensor(rms1[j % 2][:], ms2[:], rstd[j % 2][:], ALU.mult).then_inc(sig["rms1_ready"], 1)
                j = i - 2
                if within(j):
                    pool.wait_ge(sig["sums_ready"], j + 1)
                    link(pool.tensor_scalar(ms[:], sum_sq[:], 1.0 / D, None, ALU.mult))
                    if j >= 1:
                        pool.wait_ge(sig["r2_ready"], j)
                    pool.tensor_tensor(rms2[:], ms[:], half, ALU.pow).then_inc(sig["rms2_ready"], 1)

        @block.scalar
        def _(act):
            def copy_out(dst, what, j, scale=None):
                ring.await_filled(act, what, j)
                if scale is None:
                    ins = nc.scalar.activation(dst, ring.bank(what, j)[:], ACT.Copy)
                else:
                    ins = nc.scalar.activation(dst, ring.bank(what, j)[:], ACT.Copy, scale=scale)
                ring.empty(ins, what, j)

            for i in range(first, end):
                if within(i):
                    for q in range(2):
                        act.wait_ge(sig["vg_done"], 2 * i + q + 1)
                        if i >= 2 and q == 0:
                            act.wait_ge(sig["kv_done"], 2 * (i - 1))
                            act.wait_ge(sig["heads_ready"], i - 1)
                        if i == 0 and q == 0:
                            act.wait_ge(sig["v_ones"], 1)
                        vg = vg_ps[:].rearrange("p (t n) -> p t n", t=2)
                        nc.scalar.activation(v1[i % 2][:, 2 * q:2 * q + 2, 0:D], vg[:, :, 0:D], ACT.Copy)
                        nc.scalar.activation(tanh[i % 2][:, 2 * q:2 * q + 2, :], vg[:, :, D:], ACT.Tanh, scale=0.5
                                             ).then_inc(sig["vg_read"], 1)
                if within(i - 2):
                    if i - 2 >= 1:
                        ring.await_filled(act, "wo", i - 3)
                    copy_out(heads_t[:], "out_t", i - 2)
                if within(i + 1):
                    if i + 1 >= 2:
                        act.wait_ge(sig["vg_done"], 2 * i)
                    copy_out(r1_t[(i + 1) % 2][:], "r1_t", i + 1, core.norm1[:])
                if within(i):
                    act.wait_ge(sig["rope_ready"], i + 1)
                    if i >= 1:
                        act.wait_ge(sig["phi_ready"], i)
                    nc.scalar.activation(exp_qk[:], turned_qk[:], ACT.Exp)
                    nc.scalar.activation(relu_qk[:], turned_qk[:], ACT.Relu).then_inc(sig["act_done"], 1)
                if within(i - 3):
                    if i - 3 >= 1:
                        ring.await_filled(act, "logits", i - 4)
                    copy_out(r2_t[:], "r2_t", i - 3, core.norm2[:])
                if within(i - 1):
                    if i - 1 >= 1:
                        act.wait_ge(sig["num_done"], 2 * (i - 1))
                    copy_out(q_t[:], "q_t", i - 1)
                if within(i - 2):
                    j = i - 2
                    act.wait_ge(sig["a1_ready"], j + 1)
                    if j >= 1:
                        act.wait_ge(sig["rms2_ready"], j)
                    for b in range(BATCH):
                        last = nc.scalar.activation(square[:, b, :], a1[:, b, :], ACT.Square, accum_out=sum_sq[:, b:b + 1])
                    last.then_inc(sig["sums_ready"], 1)

        @block.vector
        def _(vec):
            link = Linked(vec, sig["vec_step"])
            for k in range(2):
                last = nc.vector.memset(v1[k][:, :, D:D + 1], 1.0)
            last.then_inc(sig["v_ones"], 1)
            for i in range(first, end):
                if within(i):
                    cos = core.c("cos")[:, i * DK:(i + 1) * DK]
                    sin = core.c("sin")[:, i * DK:(i + 1) * DK]
                    by_head = lambda ap: ap.rearrange("p (h d) -> p h d", d=DK)
                    for q in range(2):
                        vec.wait_ge(sig["qk_done"], 2 * i + q + 1)
                        if i >= 1 and q == 0:
                            vec.wait_ge(sig["act_done"], i)
                        two = lambda x: x[:, 2 * q:2 * q + 2, :].rearrange("p t (h d) -> p (t h) d", d=DK)
                        nc.vector.tensor_tensor(two(turned_qk), by_head(qk_ps[:]), spread(cos, 4 * HEADS, inner=False), ALU.mult)
                        nc.vector.tensor_tensor(two(sin_part), by_head(qk_ps[:]), spread(sin, 4 * HEADS, inner=False), ALU.mult
                                                ).then_inc(sig["qk_read"], 1)
                    vec.wait_ge(sig["qk_read"], 2 * i + 2)
                    split = lambda x: x[:].rearrange("p t (h s d) -> p (t h) s d", s=2, d=DK // 2)
                    nc.vector.tensor_tensor(split(turned_qk)[:, :, 0, :], split(turned_qk)[:, :, 0, :], split(sin_part)[:, :, 1, :], ALU.add)
                    nc.vector.tensor_tensor(split(turned_qk)[:, :, 1, :], split(turned_qk)[:, :, 1, :], split(sin_part)[:, :, 0, :], ALU.add
                                            ).then_inc(sig["rope_ready"], 1)
                j = i - 2
                if within(j):
                    ring.await_filled(vec, "wo", j)
                    if j >= 1:
                        vec.wait_ge(sig["sums_ready"], j)
                    ins = nc.vector.tensor_tensor(a1[:].rearrange("p b d -> p (b d)"), ring.bank("wo", j)[:],
                                                  norm[j % 4][:].rearrange("p b d -> p (b d)"), ALU.add)
                    ring.empty(ins, "wo", j)
                    ring.await_emptied(vec, "wo", j)
                    nc.vector.tensor_tensor(core.x[:, :, j, :], core.x[:, :, j, :], a1[:], ALU.add).then_inc(sig["a1_ready"], 1)
                j = i - 1
                if within(j):
                    for c in range(2):
                        vec.wait_ge(sig["kv_done"], 2 * j + c + 1)
                        if j >= 1:
                            vec.wait_ge(sig["num_done"], 2 * (j - 1) + c + 1)
                        mask = core.c("headmask").unsqueeze(1).unsqueeze(1).to_broadcast([P, 2, 2, D])
                        nc.vector.tensor_tensor(four(state[c][:, :, 0:D]), kv[:, :, :, 0:D], mask, ALU.mult)
                        col = core.c("headcol").unsqueeze(1).unsqueeze(1).to_broadcast([P, 2, 2, HEADS])
                        nc.vector.tensor_tensor(four(state[c][:, :, D:]), kv[:, :, :, D:D + 1].to_broadcast([P, 2, 2, HEADS]), col, ALU.mult
                                                ).then_inc(sig["state_ready"], 1)
                j = i + 2
                if within(j):
                    back.add(nc, vec, core.x[:, :, j, :], j)
                    statistics(nc, link, vec, core.x[:, :, j, :], stats, mean_var[j % 2], sig["stats_ready"])
                if within(i):
                    vec.wait_ge(sig["act_done"], i + 1)
                    if i >= 2:
                        vec.wait_ge(sig["kv_done"], 2 * (i - 1))
                    nc.vector.scalar_tensor_tensor(phi[i % 2][:], exp_qk[:], 1.0, relu_qk[:], ALU.min, ALU.add
                                                   ).then_inc(sig["phi_ready"], 1)
                if within(j):
                    vec.wait_ge(sig["rms1_ready"], j + 1)
                    if j >= 2:
                        ring.await_filled(vec, "r1_t", j - 2)
                    for b in range(BATCH):
                        mean = mean_var[j % 2][:, b, 0:1]
                        xb = core.x[:, b, j, :]
                        nc.vector.tensor_scalar(r1[j % 2][:, b, :], xb, mean, rms1[j % 2][:, b:b + 1], ALU.subtract, ALU.mult)
                        last = nc.vector.tensor_scalar(norm[j % 4][:, b, :], xb, mean, rstd[j % 2][:, b:b + 1], ALU.subtract, ALU.mult)
                    last.then_inc(sig["norm_ready"], 1)
                j = i - 2
                if within(j):
                    vec.wait_ge(sig["rms2_ready"], j + 1)
                    if j >= 2:
                        ring.await_filled(vec, "r2_t", j - 2)
                        vec.wait_ge(r2_stored[j % 2], 16 * (j // 2))
                    for b in range(BATCH):
                        last = nc.vector.tensor_scalar(r2[j % 2][:, b, :], a1[:, b, :], rms2[:, b:b + 1], None, ALU.mult)
                    last.then_inc(sig["r2_ready"], 1)
                j = i - 3
                if within(j):
                    ring.await_filled(vec, "logits", j)
                    ins = nc.vector.tensor_tensor(
                        core.logits[:, j:TILES:S, :], ring.bank("logits", j)[:, 0:BATCH * MOE_EXPERTS].rearrange("p (b e) -> p b e", b=BATCH),
                        spread(core.router_bias[:], BATCH, inner=False), ALU.add)
                    ring.empty(ins, "logits", j)
                j = i - 1
                if within(j):
                    vec.wait_ge(sig["num_done"], 2 * j + 2)
                    link(nc.vector.tensor_scalar(four(den[:]), num[:, :, :, D:], 2.0, 2.0 * DEN_EPS, ALU.mult, ALU.add))
                    nc.vector.reciprocal(recip[:], den[:])
                    for a in range(2):
                        last = nc.vector.scalar_tensor_tensor(
                            gated[:, 2 * a:2 * a + 2, :], tanh[j % 2][:, 2 * a:2 * a + 2, :], 1.0, num[:, a, :, 0:D], ALU.add, ALU.mult)
                    last.then_inc(sig["num_read"], 1)
                    vec.wait_ge(sig["num_read"], j + 1)
                    if j >= 1:
                        ring.await_filled(vec, "out_t", j - 1)
                    by_head = lambda ap: ap.rearrange("p b (h d) -> p (b h) d", d=DK)
                    nc.vector.tensor_tensor(by_head(heads[:]), by_head(gated[:]),
                                            recip[:].rearrange("p b h -> p (b h)").unsqueeze(2).to_broadcast([P, BATCH * HEADS, DK]), ALU.mult
                                            ).then_inc(sig["heads_ready"], 1)

        @block.tensor
        def _(pe):
            ones3 = core.ones_bf[0:3, :]

            def turn(what, j, src):
                ring.claim(pe, what, j)
                for b in range(BATCH):
                    last = nc.tensor.transpose(ring.bank(what, j)[:, b * P:(b + 1) * P], src(b), core.c("ident"))
                ring.fill(last, what, j)

            def bias(out, at, width, times):
                nc.tensor.matmul(out, ones3, core.bias3[:, at:at + width].unsqueeze(1).to_broadcast([3, times, width]),
                                 start=True, stop=False, skip_group_check=True)

            def states(j, c):
                if c == 0:
                    pe.wait_ge(sig["phi_ready"], j + 1)
                    pe.wait_ge(sig["vg_read"], 2 * j + 2)
                if 2 * j + c >= 1:
                    pe.wait_ge(sig["state_ready"], 2 * j + c)
                rows_c = slice(c * CHUNK, (c + 1) * CHUNK)
                for b in range(BATCH):
                    last = nc.tensor.matmul(kv[:, b // 2, b % 2, :], phi[j % 2][rows_c, b, D:], v1[j % 2][rows_c, b, :],
                                            start=(j == 0 and c == 0 and b % 2 == 0), stop=True, skip_group_check=True)
                last.then_inc(sig["kv_done"], 1)

            def numerators(j, c):
                pe.wait_ge(sig["state_ready"], 2 * j + c + 1)
                if c == 0:
                    ring.await_emptied(pe, "q_t", j)
                    if j >= 1:
                        pe.wait_ge(sig["num_read"], j)
                rows_c = slice(c * CHUNK, (c + 1) * CHUNK)
                for b in range(BATCH):
                    last = nc.tensor.matmul(num[rows_c, b // 2, b % 2, :], q_t[:, b * P + c * CHUNK:b * P + (c + 1) * CHUNK],
                                            state[c][:, b, :], start=True, stop=True, skip_group_check=True)
                last.then_inc(sig["num_done"], 1)

            for i in range(first, end):
                if within(i):
                    ring.await_emptied(pe, "r1_t", i)
                    for q in range(2):
                        for bank, at, done, read in ((qk_ps, 0, sig["qk_done"], sig["qk_read"]), (vg_ps, 2 * D, sig["vg_done"], sig["vg_read"])):
                            if 2 * i + q >= 1:
                                pe.wait_ge(read, 2 * i + q)
                            bias(bank[:].rearrange("p (t n) -> p t n", t=2), at, 2 * D, 2)
                            for t in range(2):
                                b = 2 * q + t
                                last = nc.tensor.matmul(bank[:, t * 2 * D:(t + 1) * 2 * D], r1_t[i % 2][:, b * P:(b + 1) * P],
                                                        core.qkvg[:].rearrange("c k n -> c (k n)")[:, at:at + 2 * D],
                                                        start=False, stop=(t == 1), skip_group_check=True)
                            last.then_inc(done, 1)
                if within(i - 2):
                    pe.wait_ge(sig["heads_ready"], i - 1)
                    turn("out_t", i - 2, lambda b: heads[:, b, :])
                if within(i + 1):
                    pe.wait_ge(sig["norm_ready"], i + 2)
                    turn("r1_t", i + 1, lambda b: r1[(i + 1) % 2][:, b, :])
                if within(i - 2):
                    ring.await_emptied(pe, "out_t", i - 2)
                    ring.claim(pe, "wo", i - 2)
                    bank = ring.bank("wo", i - 2)
                    bias(bank[:].rearrange("p (t n) -> p t n", t=BATCH), 4 * D, D, BATCH)
                    for b in range(BATCH):
                        last = nc.tensor.matmul(bank[:, b * D:(b + 1) * D], heads_t[:, b * P:(b + 1) * P], core.wo[:],
                                                start=False, stop=(b == BATCH - 1), skip_group_check=True)
                    ring.fill(last, "wo", i - 2)
                if within(i - 3):
                    pe.wait_ge(sig["r2_ready"], i - 2)
                    turn("r2_t", i - 3, lambda b: r2[(i - 3) % 2][:, b, :])
                if within(i - 1):
                    pe.wait_ge(sig["phi_ready"], i)
                    turn("q_t", i - 1, lambda b: phi[(i - 1) % 2][:, b, 0:D])
                    states(i - 1, 0)
                if within(i - 3):
                    ring.await_emptied(pe, "r2_t", i - 3)
                    ring.claim(pe, "logits", i - 3)
                    for b in range(BATCH):
                        last = nc.tensor.matmul(ring.bank("logits", i - 3)[:, b * MOE_EXPERTS:(b + 1) * MOE_EXPERTS],
                                                r2_t[:, b * P:(b + 1) * P], core.moe_router[:], start=True, stop=True)
                    ring.fill(last, "logits", i - 3)
                if within(i - 1):
                    states(i - 1, 1)
                    numerators(i - 1, 0)
                    numerators(i - 1, 1)



def moe_choices(nc, core, tag):
    with Scope(nc, tag) as s, nc.Block() as block:
        probs = s.sb("probs", [P, TILES, MOE_EXPERTS])
        same = s.sb("same", [P, TILES, MOE_EXPERTS])
        most, total, inverse = (s.sb(n, [P, TILES]) for n in ("most", "total", "inverse"))
        vec_step, shifted, exp_done = s.sem("vec_step"), s.sem("shifted"), s.sem("exp_done")

        @block.scalar
        def _(act):
            act.wait_ge(shifted, 1)
            nc.scalar.activation(probs[:], core.logits[:], ACT.Exp).then_inc(exp_done, 1)

        @block.vector
        def _(vec):
            link = Linked(vec, vec_step)
            link(nc.vector.tensor_reduce(most[:], core.logits[:], axis=AX, op=ALU.max))
            nc.vector.tensor_tensor(core.logits[:], core.logits[:], spread(most[:], MOE_EXPERTS), ALU.subtract).then_inc(shifted, 1)
            vec.wait_ge(exp_done, 1)
            link(nc.vector.tensor_reduce(total[:], probs[:], axis=AX, op=ALU.add))
            link(nc.vector.reciprocal(inverse[:], total[:]))
            link(nc.vector.tensor_tensor(probs[:], probs[:], spread(inverse[:], MOE_EXPERTS), ALU.mult))
            top_two(nc, link, probs[:], core.c("rev")[:, 0:MOE_EXPERTS],
                    [core.moe_pick[k] for k in range(2)], [core.tops[:, k, :] for k in range(2)], (same[:], most[:]))
            link(nc.vector.tensor_tensor(total[:], core.tops[:, 0, :], core.tops[:, 1, :], ALU.add))
            link(nc.vector.reciprocal(inverse[:], total[:]))
            nc.vector.tensor_tensor(core.gates[:], core.tops[:], spread(inverse[:], 2, inner=False), ALU.mult)


def moe_experts(nc, core, tag):
    half = CAPACITY // 2
    split = 3
    parts = ((0, split), (split, CAP_TILES))
    with Scope(nc, tag) as s, nc.Block() as block:
        rows = [s.sb(f"rows{k}", [P, CAP_TILES, D]) for k in range(2)]
        rows_t = [s.sb(f"rows_t{k}", [P, CAPACITY]) for k in range(2)]
        hid = [s.sb(f"hid{k}", [P, HID_CHUNKS, CAPACITY]) for k in range(2)]
        out = [s.sb(f"out{k}", [P, CAP_TILES, D]) for k in range(2)]
        t_ps = [s.ps(f"t_ps{k}") for k in range(2)]
        hid_ps = [s.ps(f"hid_ps{k}") for k in range(4)]
        out_ps = [s.ps(f"out_ps{k}") for k in range(2)]
        arrived = [s.sem(f"arrived{k}") for k in range(2)]
        stored = [s.sem(f"stored{k}") for k in range(2)]
        turned, turn_copied, hid_done, gelu_done, out_done, out_copied = (
            s.sem(n) for n in ("turned", "turn_copied", "hid_done", "gelu_done", "out_done", "out_copied"))
        stores = core.moe_out_rows[0:MOE_ROWS, :].rearrange("(e t p) d -> e p t d", p=P, t=CAP_TILES)
        units = [(c, h) for c in range(HID_CHUNKS) for h in range(2)]

        @block.gpsimd
        def _(pool):
            for e in range(MOE_EXPERTS):
                if e >= 2:
                    pool.wait_ge(turned, 2 * (e - 1))
                for t in range(CAP_TILES):
                    n = e * CAP_TILES + t
                    pool.indirect_dma_start(
                        out=rows[e % 2][:, t, :], out_offset=None, in_=core.moe_rows,
                        in_offset=bass.IndirectOffsetOnAxis(ap=core.gather_id[:, n:n + 1], axis=0),
                    ).then_inc(arrived[e % 2], 16)

        @block.tensor
        def _(pe):
            def turn(e):
                pe.wait_ge(arrived[e % 2], 16 * CAP_TILES * (e // 2 + 1))
                for k, (lo, hi) in enumerate(parts):
                    if e >= 1:
                        pe.wait_ge(turn_copied, 2 * (e - 1) + k + 1)
                    for t in range(lo, hi):
                        last = nc.tensor.transpose(t_ps[k][:, (t - lo) * P:(t - lo + 1) * P], rows[e % 2][:, t, :], core.c("ident"))
                    last.then_inc(turned, 1)

            turn(0)
            for e in range(MOE_EXPERTS):
                pe.wait_ge(turn_copied, 2 * e + 2)
                for u, (c, h) in enumerate(units):
                    n = len(units) * e + u
                    if n >= 4:
                        pe.wait_ge(gelu_done, n - 3)
                    nc.tensor.matmul(hid_ps[n % 4][:, 0:half], core.w1[:, e, c * P:(c + 1) * P],
                                     rows_t[e % 2][:, h * half:(h + 1) * half], start=True, stop=True).then_inc(hid_done, 1)
                if e + 1 < MOE_EXPERTS:
                    turn(e + 1)
                pe.wait_ge(gelu_done, len(units) * (e + 1))
                for k, (lo, hi) in enumerate(parts):
                    if e >= 1:
                        pe.wait_ge(out_copied, 2 * (e - 1) + k + 1)
                    for t in range(lo, hi):
                        dst = out_ps[k][:, (t - lo) * D:(t - lo + 1) * D]
                        nc.tensor.matmul(dst, core.ones_bf[0:3, :], core.bias3[:, 5 * D + e * D:5 * D + (e + 1) * D], start=True, stop=False)
                        for c in range(HID_CHUNKS):
                            last = nc.tensor.matmul(dst, hid[e % 2][:, c, t * P:(t + 1) * P], core.w2[:, e, c, :],
                                                    start=False, stop=(c == HID_CHUNKS - 1))
                    last.then_inc(out_done, 1)

        @block.scalar
        def _(act):
            for e in range(MOE_EXPERTS):
                for u, (c, h) in enumerate(units):
                    n = len(units) * e + u
                    act.wait_ge(hid_done, n + 1)
                    if u == 0 and e >= 2:
                        act.wait_ge(out_done, 2 * (e - 1))
                    bias = e * HID_CHUNKS + c
                    nc.scalar.activation(hid[e % 2][:, c, h * half:(h + 1) * half], hid_ps[n % 4][:, 0:half], ACT.Gelu,
                                         bias=core.b1[:, bias:bias + 1]).then_inc(gelu_done, 1)

        @block.vector
        def _(vec):
            def copy_turned(e):
                for k, (lo, hi) in enumerate(parts):
                    vec.wait_ge(turned, 2 * e + k + 1)
                    if e >= 2 and k == 0:
                        vec.wait_ge(hid_done, len(units) * (e - 1))
                    nc.vector.tensor_scalar(rows_t[e % 2][:, lo * P:hi * P], t_ps[k][:, 0:(hi - lo) * P], core.norm2[:], None, ALU.mult
                                            ).then_inc(turn_copied, 1)

            copy_turned(0)
            for e in range(MOE_EXPERTS):
                if e + 1 < MOE_EXPERTS:
                    copy_turned(e + 1)
                for k, (lo, hi) in enumerate(parts):
                    vec.wait_ge(out_done, 2 * e + k + 1)
                    if k == 0 and e >= 2:
                        vec.wait_ge(stored[e % 2], 16 * (e // 2))
                    nc.vector.tensor_copy(out[e % 2][:, lo:hi, :], out_ps[k][:, 0:(hi - lo) * D].rearrange("p (t d) -> p t d", d=D)
                                          ).then_inc(out_copied, 1)

        @block.sync
        def _(sp):
            for e in range(MOE_EXPERTS):
                sp.wait_ge(out_copied, 2 * e + 2)
                sp.dma_start(stores[e], out[e % 2][:]).then_inc(stored[e % 2], 16)
            for k in range(2):
                sp.wait_ge(stored[k], 16 * (MOE_EXPERTS // 2))


def ffn_last(nc, core, tag, combine, out):
    out_steps = out.rearrange("b (j p) d -> j p b d", p=P)
    with Scope(nc, tag) as s, nc.Block() as block:
        back = Returned(s, *combine)
        out_stored = s.sem("out_stored")

        @block.gpsimd
        def _(pool):
            for j in range(SEQ_TILES):
                back.gather(pool, j)

        @block.vector
        def _(vec):
            for j in range(SEQ_TILES):
                back.add(nc, vec, core.x[:, :, j, :], j)

        @block.sync
        def _(sp):
            for j in range(SEQ_TILES):
                sp.wait_ge(back.used, j + 1)
                sp.dma_start(out_steps[j], core.x[:, :, j, :]).then_inc(out_stored, 16)
            sp.wait_ge(out_stored, 16 * SEQ_TILES)



def allocate(nc, stack):
    core = Core()

    def sb(name, shape, dt=F32):
        return stack.enter_context(nc.sbuf_tensor(f"core_{name}", shape, dt))

    core.x = sb("x", [P, BATCH, SEQ_TILES, D])
    core.const = sb("const", [P, CONST_COLS])
    core.gate_up = sb("gate_up", [P, FFN_EXPERTS, 2 * FFN_HID])
    core.down = sb("down", [P, FFN_EXPERTS, D])
    core.ffn_router = sb("ffn_router", [P, FFN_EXPERTS])
    core.shared_gate = sb("shared_gate", [P, SHARED])
    core.shared_up = sb("shared_up", [P, SHARED])
    core.shared_down = sb("shared_down", [P, 2, D])
    core.qkvg = sb("qkvg", [P, 4, D])
    core.wo = sb("wo", [P, D])
    core.norm1 = sb("norm1", [P, 1])
    core.norm2 = sb("norm2", [P, 1])
    core.moe_router = sb("moe_router", [P, MOE_EXPERTS])
    core.router_bias = sb("router_bias", [P, MOE_EXPERTS])
    core.b1 = sb("b1", [P, MOE_EXPERTS * HID_CHUNKS])
    core.w1 = sb("w1", [P, MOE_EXPERTS, MOE_HID])
    core.w2 = sb("w2", [P, MOE_EXPERTS, HID_CHUNKS, D])
    core.bias_cols = 5 * D + MOE_EXPERTS * D
    core.bias3 = sb("bias3", [3, core.bias_cols], BF16)
    core.before16 = sb("before16", [P, P], F16)
    core.ones16 = sb("ones16", [P, P], F16)
    core.iota16 = sb("iota16", [P, P], F16)
    core.ones_bf = sb("ones_bf", [3, P], BF16)
    core.pick_all = stack.enter_context(nc.sbuf_tensor("core_pick", [P, 2, TILES * FFN_EXPERTS], F32))
    core.tops = sb("tops", [P, 2, TILES])
    core.logits = sb("logits", [P, TILES, MOE_EXPERTS])
    core.gates = sb("gates", [P, 2, TILES])
    core.back_slot = sb("back_slot", [P, 2, TILES], I32)
    core.gather_id = sb("gather_id", [P, FFN_TILES], I32)
    core.expert_ids = sb("expert_ids", [1, FFN_TILES], I32)
    core.pick = [core.pick_all[:, k, :].rearrange("p (t e) -> p t e", e=FFN_EXPERTS) for k in range(2)]
    core.moe_pick = [core.pick_all[:, k, 0:TILES * MOE_EXPERTS].rearrange("p (t e) -> p t e", e=MOE_EXPERTS) for k in range(2)]
    core.c = lambda name: core.const[:, CONST_AT[name][0]:CONST_AT[name][1]]
    core.norm_rows = nc.dram_tensor("norm_rows", [TOKENS, D], F32, kind="Internal").ap()
    core.ffn_out_rows = nc.dram_tensor("ffn_out_rows", [FFN_TILES * P, D], F32, kind="Internal").ap()
    core.moe_rows = nc.dram_tensor("moe_rows", [TOKENS, D], F32, kind="Internal").ap()
    core.moe_out_rows = nc.dram_tensor("moe_out_rows", [MOE_ROWS + P, D], F32, kind="Internal").ap()
    return core


def build(nc, w, x, out):
    with ExitStack() as stack:
        core = allocate(nc, stack)
        load_all(nc, core, w, x)
        ffn_back = (core.ffn_out_rows, core.back_slot, core.gates)
        moe_back = (core.moe_out_rows, core.back_slot, core.gates)
        ffn_front(nc, core, "front1")
        rank(nc, core, "rank1", core.pick, FFN_EXPERTS, FFN_TILES)
        ffn_experts(nc, core, "ffn1")
        attention(nc, core, "attn", ffn_back)
        moe_choices(nc, core, "choices")
        rank(nc, core, "rank2", core.moe_pick, MOE_EXPERTS, MOE_TILES, CAPACITY)
        moe_experts(nc, core, "moe")
        ffn_front(nc, core, "front3", moe_back)
        rank(nc, core, "rank3", core.pick, FFN_EXPERTS, FFN_TILES)
        ffn_experts(nc, core, "ffn3")
        ffn_last(nc, core, "last", ffn_back, out)


PLAIN = dict(
    wq="Wq", wk="Wk", wv="Wv", wg="Wg", wo="Wo", bq="bq", bk="bk", bv="bv", bg="bg", bo="bo",
    norm1="norm1_scale", norm2="norm2_scale", moe_router="router_W", router_bias="router_b",
    w1="W1", b1="b1", w2="W2", b2="b2",
)
FFN_PLAIN = dict(gate_up="gate_up_w", down="down_w")
FFN_TURNED = dict(ffn_router="router_w", shared_gate="shared_gate_w", shared_up="shared_up_w", shared_down="shared_down_w")


def host_arrays(inputs):
    arrays = {"x": np.ascontiguousarray(inputs["L0_attn_x"]), "const": constants()}
    for name, given in PLAIN.items():
        arrays[name] = np.ascontiguousarray(inputs[f"L0_attn_{given}"])
    b1 = arrays["b1"].reshape(MOE_EXPERTS * HID_CHUNKS, P)
    arrays["b1"] = np.ascontiguousarray(b1.T)
    for name, given in FFN_PLAIN.items():
        arrays[name] = np.ascontiguousarray(inputs[f"L0_ffn_{given}"])
    for name, given in FFN_TURNED.items():
        arrays[name] = np.ascontiguousarray(np.asarray(inputs[f"L0_ffn_{given}"]).T)
    return arrays


def kernel(**inputs):
    import concourse.bacc as bacc
    from concourse.bass_utils import run_bass_kernel_spmd

    nc = bacc.Bacc("TRN2", target_bir_lowering=False, num_devices=1)
    arrays = host_arrays(inputs)
    w = {name: nc.dram_tensor(f"in_{name}", a.shape, mybir.dt.from_np(a.dtype), kind="ExternalInput").ap()
         for name, a in arrays.items()}
    x = w.pop("x")
    out = nc.dram_tensor("result", list(x.shape), F32, kind="ExternalOutput").ap()
    build(nc, w, x, out)
    got = run_bass_kernel_spmd(nc, [{f"in_{name}": a for name, a in arrays.items()}], core_ids=[0])
    return got.results[0]["result"]
```

```python
from contextlib import ExitStack

import numpy as np

import concourse.bass as bass
from concourse import mybir

P = 128
D = 128
BATCH = 4
SEQ_TILES = 8
TILES = BATCH * SEQ_TILES
TOKENS = TILES * P
LN_EPS = 1e-5

FFN_EXPERTS = 16
FFN_HID = 128
SHARED = 256
FFN_TILES = 2 * TOKENS // P + FFN_EXPERTS - 1
PAIRS = (FFN_TILES + 1) // 2

MOE_EXPERTS = 8
MOE_HID = 512
HID_CHUNKS = MOE_HID // P
CAPACITY = int(1.25 * (TOKENS / MOE_EXPERTS))
CAP_TILES = CAPACITY // P
MOE_TILES = MOE_EXPERTS * CAP_TILES
MOE_ROWS = MOE_TILES * P
assert CAP_TILES * P == CAPACITY

HEADS = 16
DK = D // HEADS
CHUNK = 64
FRONT_AHEAD = 6
LATE = 2
ATTENTION_AHEAD = (3, 5, 5, 7, 8, 8, 8, 8)
BIAS_COLS = 5 * D + MOE_EXPERTS * D
DEN_EPS = 1e-6

F32 = mybir.dt.float32
BF16 = mybir.dt.bfloat16
F16 = mybir.dt.float16
I32 = mybir.dt.int32
ALU = mybir.AluOpType
ACT = mybir.ActivationFunctionType
AX = mybir.AxisListType.X

CONST_WIDTHS = dict(
    ident=P, rev=FFN_EXPERTS, minus_half=BATCH,
    restart=FFN_EXPERTS * TILES, token_id=TILES, part=1, ones=FFN_EXPERTS,
    expert_base=MOE_EXPERTS, headmask=D, headcol=HEADS, cos=SEQ_TILES * DK, sin=SEQ_TILES * DK,
)
CONST_AT = {}
_at = 0
for _name, _width in CONST_WIDTHS.items():
    CONST_AT[_name] = (_at, _at + _width)
    _at += _width
CONST_COLS = _at
CONST_FIRST = CONST_AT["restart"][0]
ID_SHIFT = TOKENS // 2
FAR = float(2 ** 20)


def constants():
    p = np.arange(P)
    c = {}
    c["ident"] = np.eye(P)
    c["headmask"] = (p[:, None] // DK == np.arange(D)[None] // DK)
    c["headcol"] = (p[:, None] // DK == np.arange(HEADS)[None])
    c["ones"] = np.ones((P, FFN_EXPERTS))
    c["rev"] = np.tile(FFN_EXPERTS - np.arange(FFN_EXPERTS), (P, 1))
    c["restart"] = np.tile((np.arange(FFN_EXPERTS * TILES) % TILES) != 0, (P, 1))
    c["token_id"] = P * np.arange(TILES)[None] + p[:, None] - ID_SHIFT
    c["part"] = p[:, None]
    c["expert_base"] = np.tile(CAPACITY * np.arange(MOE_EXPERTS), (P, 1))
    half = DK // 2
    inv = (1.0 / 10000.0 ** (np.arange(half, dtype=np.float32) / half)).astype(np.float32)
    angle = (np.arange(SEQ_TILES * P, dtype=np.float32)[:, None] * inv[None]).astype(np.float32)
    cos = np.cos(angle).reshape(SEQ_TILES, P, half).transpose(1, 0, 2)
    sin = np.sin(angle).reshape(SEQ_TILES, P, half).transpose(1, 0, 2)
    c["cos"] = np.concatenate([cos, cos], -1).reshape(P, -1)
    c["sin"] = np.concatenate([sin, -sin], -1).reshape(P, -1)
    c["minus_half"] = np.full((P, BATCH), -0.5)
    return np.concatenate([c[n].astype(np.float32) for n in CONST_WIDTHS], axis=1)


def constants16():
    p = np.arange(P)
    return np.concatenate([-1.0 * (p[:, None] >= p[None]), np.tile(p, (P, 1))], axis=1).astype(np.float16)


class Core:
    pass


class Linked:

    def __init__(self, eng, done):
        self.eng, self.done, self.n = eng, done, 0

    def __call__(self, ins):
        self.n += 1
        ins.then_inc(self.done, 1)
        self.eng.wait_ge(self.done, self.n)


class Scope:
    sems = []

    def __init__(self, nc, tag):
        self.nc, self.tag, self.stack = nc, tag, ExitStack()

    def __enter__(self):
        return self

    def __exit__(self, *a):
        self.stack.close()

    def sb(self, name, shape, dt=F32):
        return self.stack.enter_context(self.nc.sbuf_tensor(f"{self.tag}_{name}", shape, dt))

    def ps(self, name, shape=(P, 512), dt=F32):
        return self.stack.enter_context(self.nc.psum_tensor(f"{self.tag}_{name}", list(shape), dt))

    def sem(self, name):
        Scope.sems.append(self.nc.alloc_semaphore(f"{self.tag}_{name}"))
        return Scope.sems[-1]


def free_semaphores(nc):
    nc.clear_and_free_semaphores(Scope.sems)
    Scope.sems = []
    nc.all_engine_barrier()


def spread(ap, n, inner=True):
    m = ap.shape[1]
    return ap.unsqueeze(2).to_broadcast([P, m, n]) if inner else ap.unsqueeze(1).to_broadcast([P, n, m])



def load_first(sp, core, w, x):
    x_steps = x.rearrange("b (j p) d -> j p b d", p=P)
    sp.dma_start(core.x[:, :, 0, :], x_steps[0]).then_inc(core.x_loaded[0], 16)
    sp.dma_start(core.const[:, 0:CONST_FIRST], w["const"][:, 0:CONST_FIRST]).then_inc(core.const_loaded, 16)
    sp.dma_start(core.x[:, :, 1, :], x_steps[1]).then_inc(core.x_loaded[1], 16)
    for dst, src in (
        (core.shared_gate[:], w["shared_gate"]),
        (core.shared_up[:], w["shared_up"]),
        (core.ffn_router[:], w["ffn_router"]),
        (core.shared_down[:], w["shared_down"].rearrange("(h s) c -> s h c", s=P)),
    ):
        sp.dma_start(dst, src).then_inc(core.shared_loaded, 16)
    for j in range(2, SEQ_TILES):
        sp.dma_start(core.x[:, :, j, :], x_steps[j]).then_inc(core.x_loaded[j], 16)
    sp.dma_start(core.const16[:], w["const16"]).then_inc(core.rank_loaded, 16)
    sp.dma_start(core.const[:, CONST_FIRST:], w["const"][:, CONST_FIRST:]).then_inc(core.rank_loaded, 16)


def load_rest(sp, core, w):
    for dst, src in (
        (core.gate_up[:], w["gate_up"].rearrange("e c h -> c e h")),
        (core.down[:], w["down"].rearrange("e h c -> h e c")),
    ):
        sp.dma_start(dst, src).then_inc(core.experts_loaded, 16)
    for k, name in enumerate(("bq", "bk", "bv", "bg", "bo")):
        sp.dma_start(core.bias_row[:, k * D:(k + 1) * D], w[name].rearrange("(a n) -> a n", a=1)
                     ).then_inc(core.bias_loaded, 16)
    sp.dma_start(core.bias_row[:, 5 * D:], w["b2"].rearrange("(a e) n -> a (e n)", a=1)).then_inc(core.bias_loaded, 16)
    for dst, src in (
        (core.qkvg[:, 0, :], w["wq"]), (core.qkvg[:, 1, :], w["wk"]),
        (core.qkvg[:, 2, :], w["wv"]), (core.qkvg[:, 3, :], w["wg"]),
        (core.wo[:], w["wo"]),
        (core.norm1[:], w["norm1"].rearrange("(c a) -> c a", a=1)),
        (core.norm2[:], w["norm2"].rearrange("(c a) -> c a", a=1)),
        (core.moe_router[:], w["moe_router"]),
        (core.router_bias[:], w["router_bias"].rearrange("(a e) -> a e", a=1).to_broadcast([P, MOE_EXPERTS])),
    ):
        sp.dma_start(dst, src).then_inc(core.attention_loaded, 16)
    sp.dma_start(core.b1[:], w["b1"]).then_inc(core.moe_loaded, 16)
    for e in range(MOE_EXPERTS):
        sp.dma_start(core.w1[:, e, :], w["w1"][e]).then_inc(core.moe_loaded, 16)
        sp.dma_start(core.w2[:, e, :, :], w["w2"][e].rearrange("(k p) c -> p k c", p=P)).then_inc(core.moe_loaded, 16)



def statistics(nc, link, vec, x, stats, mean_var, ready):
    for b in range(BATCH):
        last = nc.vector.bn_stats(stats[:, b, :], x[:, b, :])
    link(last)
    for b in range(BATCH):
        last = nc.vector.bn_aggr(mean_var[:, b, :], stats[:, b, :])
    last.then_inc(ready, 1)


def top_two(nc, link, values, rev, one_hots, tops, scratch):
    same, first = scratch
    shape = list(values.shape)
    by_row = lambda ap: ap.unsqueeze(len(shape) - 1).to_broadcast(shape)
    rank = rev
    while len(rank.shape) < len(shape):
        rank = rank.unsqueeze(1)
    rank = rank.to_broadcast(shape)
    for k in range(2):
        link(nc.vector.tensor_reduce(tops[k], values, axis=AX, op=ALU.max))
        link(nc.vector.tensor_tensor(same, values, by_row(tops[k]), ALU.is_equal))
        link(nc.vector.tensor_tensor(same, same, rank, ALU.mult))
        link(nc.vector.tensor_reduce(first, same, axis=AX, op=ALU.max))
        link(nc.vector.tensor_tensor(one_hots[k], rank, by_row(first), ALU.is_equal))
        if k == 0:
            link(nc.vector.scalar_tensor_tensor(values, one_hots[0], -1e30, values, ALU.mult, ALU.add))


class Returned:

    def __init__(self, s, rows, back_slot, gates):
        self.rows, self.back_slot, self.gates = rows, back_slot, gates
        self.got = [s.sb(f"back{k}", [P, 2, BATCH, D]) for k in range(2)]
        self.arrived = [s.sem(f"back_arrived{k}") for k in range(2)]
        self.started = 0
        self.used, self.half = s.sem("back_used"), s.sem("back_half")

    def gather_until(self, pool, count):
        for n in range(self.started, min(count, 2 * BATCH * SEQ_TILES)):
            j, (k, b) = n // (2 * BATCH), divmod(n % (2 * BATCH), BATCH)
            if j >= 2 and k == b == 0:
                pool.wait_ge(self.used, j - 1)
            t = SEQ_TILES * b + j
            pool.indirect_dma_start(
                out=self.got[j % 2][:, k, b, :], out_offset=None, in_=self.rows,
                in_offset=bass.IndirectOffsetOnAxis(ap=self.back_slot[:, k, t:t + 1], axis=0),
            ).then_inc(self.arrived[j % 2], 16)
        self.started = max(self.started, count)

    def add(self, nc, vec, x, j):
        vec.wait_ge(self.arrived[j % 2], 16 * 2 * BATCH * (j // 2 + 1))
        for k, done in enumerate((self.half, self.used)):
            for b in range(BATCH):
                t = SEQ_TILES * b + j
                last = nc.vector.scalar_tensor_tensor(
                    x[:, b, :], self.got[j % 2][:, k, b, :], self.gates[:, k, t:t + 1], x[:, b, :], ALU.mult, ALU.add)
            last.then_inc(done, 1)
            vec.wait_ge(done, j + 1)


def shared_down_of(nc, core, hid, down_ps):
    for b in range(BATCH):
        for h in range(2):
            last = nc.tensor.matmul(down_ps[:, b * D:(b + 1) * D], hid[:, h, b * P:(b + 1) * P],
                                    core.shared_down[:, h, :], start=(h == 0), stop=(h == 1))
    return last



def ffn_front(nc, core, tag, combine=None, load=None):
    shared_steps = 0 if combine else SEQ_TILES - LATE
    lead = 1 if combine else 2
    choices_after = {2: (0, 2), 4: (2, 5), 6: (5, 7), 7: (7, 8)} if combine else {1: (0, 2), 3: (2, 4), 7: (4, 8)}
    with Scope(nc, tag) as s, nc.Block() as block:
        norm = [s.sb(f"norm{k}", [P, BATCH, D]) for k in range(2)]
        if shared_steps:
            gate = s.sb("gate", [P, 2, BATCH * P])
            hid = [s.sb(f"hid{k}", [P, 2, BATCH * P]) for k in range(2)]
        stats = s.sb("stats", [P, BATCH, 6])
        mean_var = [s.sb(f"mean_var{k}", [P, BATCH, 2]) for k in range(2)]
        var_eps = s.sb("var_eps", [P, BATCH])
        rstd = [s.sb(f"rstd{k}", [P, BATCH]) for k in range(2)]
        logits = s.sb("logits", [P, BATCH, SEQ_TILES, FFN_EXPERTS])
        same = s.sb("same", [P, BATCH, SEQ_TILES, FFN_EXPERTS])
        first = s.sb("first", [P, BATCH, SEQ_TILES])
        t_ps = [s.ps(f"t{k}") for k in range(2)]
        logits_ps, down_ps = s.ps("logits_ps"), s.ps("down_ps")
        gate_ps = [s.ps(f"gate_ps{k}") for k in range(2)]
        up_ps = [s.ps(f"up_ps{k}") for k in range(2)]

        stats_ready, rstd_ready, pool_step, vec_step = (s.sem(n) for n in ("stats_ready", "rstd_ready", "pool_step", "vec_step"))
        norm_ready, turned, turn_copied, logits_done, logits_read = (
            s.sem(n) for n in ("norm_ready", "turned", "turn_copied", "logits_done", "logits_read"))
        gate_done, up_done, silu_done, hid_ready, down_done, x_updated = (
            s.sem(n) for n in ("gate_done", "up_done", "silu_done", "hid_ready", "down_done", "x_updated"))
        stored = [s.sem(f"stored{k}") for k in range(2)]
        back = Returned(s, *combine) if combine else None
        rows = core.norm_rows.rearrange("(b j p) d -> j p b d", p=P, j=SEQ_TILES)

        @block.sync
        def _(sp):
            if load:
                load(sp)
            for j in range(SEQ_TILES):
                sp.wait_ge(norm_ready, j + 1)
                sp.dma_start(rows[j], norm[j % 2][:]).then_inc(stored[j % 2], 16)
            for k in range(2):
                sp.wait_ge(stored[k], 16 * (SEQ_TILES // 2))

        @block.gpsimd
        def _(pool):
            link = Linked(pool, pool_step)
            pool.wait_ge(core.const_loaded, 16)
            for j in range(SEQ_TILES):
                if back:
                    ahead = FRONT_AHEAD if j < SEQ_TILES - 2 else 2 * BATCH
                    back.gather_until(pool, 2 * BATCH * (j + 1) + ahead)
                pool.wait_ge(stats_ready, j + 1)
                link(pool.tensor_scalar(var_eps[:], mean_var[j % 2][:, :, 1], LN_EPS, None, ALU.add))
                if j >= 2:
                    pool.wait_ge(norm_ready, j - 1)
                pool.tensor_tensor(rstd[j % 2][:], var_eps[:], core.c("minus_half"), ALU.pow).then_inc(rstd_ready, 1)

        @block.scalar
        def _(act):
            def copy_turned(j):
                act.wait_ge(turned, j + 1)
                nc.scalar.activation(core.norm_t[:, j, :], t_ps[j % 2][:], ACT.Copy).then_inc(turn_copied, 1)

            for i in range(-1, SEQ_TILES):
                if lead == 2 and i + 1 < SEQ_TILES:
                    copy_turned(i + 1)
                if i >= 0:
                    act.wait_ge(logits_done, i + 1)
                    nc.scalar.activation(logits[:, :, i, :], logits_ps[:, 0:BATCH * FFN_EXPERTS].rearrange("p (b e) -> p b e", b=BATCH),
                                         ACT.Copy).then_inc(logits_read, 1)
                    for h in range(2 if i < shared_steps else 0):
                        act.wait_ge(gate_done, 2 * i + h + 1)
                        if i >= 1:
                            act.wait_ge(hid_ready, 2 * (i - 1) + h + 1)
                        nc.scalar.activation(gate[:, h, :], gate_ps[h][:], ACT.Silu).then_inc(silu_done, 1)
                if lead == 1 and i + 1 < SEQ_TILES:
                    copy_turned(i + 1)
            if shared_steps:
                for n in range(2 * LATE):
                    act.wait_ge(gate_done, 2 * shared_steps + n + 1)
                    nc.scalar.activation(core.late_gate[:, n, :], gate_ps[n % 2][:], ACT.Silu).then_inc(silu_done, 1)

        @block.vector
        def _(vec):
            link = Linked(vec, vec_step)
            vec.wait_ge(core.const_loaded, 16)

            def hidden(i, h):
                vec.wait_ge(silu_done, 2 * i + h + 1)
                vec.wait_ge(up_done, 2 * i + h + 1)
                if h == 0 and i >= 2:
                    vec.wait_ge(down_done, i - 1)
                nc.vector.tensor_tensor(hid[i % 2][:, h, :], gate[:, h, :], up_ps[h][:], ALU.mult).then_inc(hid_ready, 1)

            def update_x(q):
                vec.wait_ge(down_done, q + 1)
                xq = core.x[:, :, q, :]
                nc.vector.scalar_tensor_tensor(
                    xq, down_ps[:].rearrange("p (b d) -> p b d", d=D), 0.5, xq, ALU.mult, ALU.add
                ).then_inc(x_updated, 1)

            def measure(j):
                xj = core.x[:, :, j, :]
                vec.wait_ge(core.x_loaded[j], 16)
                if back:
                    back.add(nc, vec, xj, j)
                statistics(nc, link, vec, xj, stats, mean_var[j % 2], stats_ready)

            def normalise(j):
                vec.wait_ge(rstd_ready, j + 1)
                if j >= 2:
                    vec.wait_ge(turned, j - 1)
                    vec.wait_ge(stored[j % 2], 16 * (j // 2))
                for b in range(BATCH):
                    last = nc.vector.tensor_scalar(
                        norm[j % 2][:, b, :], core.x[:, b, j, :], mean_var[j % 2][:, b, 0:1],
                        rstd[j % 2][:, b:b + 1], ALU.subtract, ALU.mult)
                last.then_inc(norm_ready, 1)

            def choose(begin, end):
                here = slice(begin, end)
                vec.wait_ge(logits_read, end)
                top_two(nc, link, logits[:, :, here, :], core.c("rev"),
                        [core.pick[k].rearrange("p (b j) e -> p b j e", b=BATCH)[:, :, here, :] for k in range(2)],
                        [core.tops[:, k, :].rearrange("p (b j) -> p b j", b=BATCH)[:, :, here] for k in range(2)],
                        (same[:, :, here, :], first[:, :, here]))

            for i in range(-lead, max(SEQ_TILES, shared_steps + 2)):
                if i == SEQ_TILES - 1:
                    choose(*choices_after[i])
                if 0 <= i - 2 < shared_steps:
                    update_x(i - 2)
                if i + lead < SEQ_TILES:
                    measure(i + lead)
                if 0 <= i < shared_steps:
                    hidden(i, 0)
                if i + lead < SEQ_TILES:
                    normalise(i + lead)
                if 0 <= i < shared_steps:
                    hidden(i, 1)
                if i in choices_after and i < SEQ_TILES - 1:
                    choose(*choices_after[i])

        @block.tensor
        def _(pe):
            pe.wait_ge(core.const_loaded, 16)

            def turn(j):
                pe.wait_ge(norm_ready, j + 1)
                if j >= 2:
                    pe.wait_ge(turn_copied, j - 1)
                for b in range(BATCH):
                    last = nc.tensor.transpose(t_ps[j % 2][:, b * P:(b + 1) * P], norm[j % 2][:, b, :], core.c("ident"))
                last.then_inc(turned, 1)

            def down(j):
                pe.wait_ge(hid_ready, 2 * (j + 1))
                if j >= 1:
                    pe.wait_ge(x_updated, j)
                shared_down_of(nc, core, hid[j % 2], down_ps).then_inc(down_done, 1)

            for i in range(-1, SEQ_TILES):
                if lead == 2 and i + 1 < SEQ_TILES:
                    turn(i + 1)
                if 0 <= i < SEQ_TILES:
                    pe.wait_ge(turn_copied, i + 1)
                    pe.wait_ge(core.shared_loaded, 16 * 4)
                    if i >= 1:
                        pe.wait_ge(logits_read, i)
                    for b in range(BATCH):
                        last = nc.tensor.matmul(
                            logits_ps[:, b * FFN_EXPERTS:(b + 1) * FFN_EXPERTS], core.norm_t[:, i, b * P:(b + 1) * P],
                            core.ffn_router[:], start=True, stop=True)
                    last.then_inc(logits_done, 1)
                    for h in range(2 if i < shared_steps else 0):
                        if i >= 1:
                            pe.wait_ge(silu_done, 2 * (i - 1) + h + 1)
                        nc.tensor.matmul(gate_ps[h][:], core.shared_gate[:, h * P:(h + 1) * P], core.norm_t[:, i, :],
                                         start=True, stop=True).then_inc(gate_done, 1)
                        if i >= 1:
                            pe.wait_ge(hid_ready, 2 * (i - 1) + h + 1)
                        nc.tensor.matmul(up_ps[h][:], core.shared_up[:, h * P:(h + 1) * P], core.norm_t[:, i, :],
                                         start=True, stop=True).then_inc(up_done, 1)
                if 1 <= i < shared_steps:
                    down(i - 1)
                if lead == 1 and i + 1 < SEQ_TILES:
                    turn(i + 1)
            if shared_steps:
                down(shared_steps - 1)
                for n in range(2 * LATE):
                    pe.wait_ge(silu_done, 2 * shared_steps + n - 1)
                    nc.tensor.matmul(gate_ps[n % 2][:], core.shared_gate[:, n % 2 * P:(n % 2 + 1) * P],
                                     core.norm_t[:, shared_steps + n // 2, :], start=True, stop=True).then_inc(gate_done, 1)



def rank(nc, core, tag, pick, experts, tiles, capacity=None, load=None, late=()):
    cells = experts * TILES
    choices = 2 * TILES
    per_group = 8
    groups = choices // per_group
    pool_groups, act_groups = (1, 3, 6), (0, 2, 4, 5, 7)
    with Scope(nc, tag) as s, nc.Block() as block:
        both = s.sb("both", [P, experts, TILES], F16)
        upto = s.sb("upto", [P, experts, TILES])
        place = s.sb("place", [P, experts, TILES])
        work = s.sb("work", [P, experts, TILES])
        used_tiles, ends, base = (s.sb(n, [P, experts]) for n in ("used_tiles", "ends", "base"))
        rounded = s.sb("rounded", [P, experts], I32)
        picked = [s.sb(f"picked{k}", [P, TILES, experts]) for k in range(2)]
        place_ready, picked_ready, pool_picked = s.sem("place_ready"), s.sem("picked_ready"), s.sem("pool_picked")
        slot = s.sb("slot", [P, 2, TILES])
        slot_int, hi_int, lo_int = (s.sb(n, [P, choices], I32) for n in ("slot_int", "hi_int", "lo_int"))
        clamped = s.sb("clamped", [P, 2, TILES])
        hi, lo = s.sb("hi", [P, choices]), s.sb("lo", [P, choices])
        lo_hot = [s.sb(f"lo_hot{k}", [P, per_group, P], F16) for k in range(2)]
        hi_hot = [s.sb(f"hi_hot{g}", [P, per_group, tiles], F16) for g in range(groups)]
        distance = [s.sb(f"distance{k}", [P, per_group, tiles], F16) for k in range(2)]
        minus_hi = s.sb("minus_hi", [P, choices])
        whose = s.sb("whose", [P, 1])
        tanh = s.sb("tanh", [P, 2, TILES])
        behind_ps, total_ps, token_ps, whose_ps = (s.ps(n) for n in ("behind_ps", "total_ps", "token_ps", "whose_ps"))
        if late:
            halves = [(j, h) for j in late for h in range(2)]
            hid = s.sb("hid", [P, len(halves), BATCH * P])
            up_ps, down_ps = [s.ps(f"up_ps{k}") for k in range(2)], s.ps("down_ps")
            up_done, hid_ready, down_done, x_updated = (s.sem(n) for n in ("up_done", "hid_ready", "down_done", "x_updated"))
        both_ready, counted, vec_step, hi_ready, lo_ready, hot_used, tokens_done = (
            s.sem(n) for n in ("both_ready", "counted", "vec_step", "hi_ready", "lo_ready", "hot_used", "tokens_done"))
        minus_hi_ready, act_step, act_hi_hot, pool_hi_hot = (s.sem(n) for n in ("minus_hi_ready", "act_step", "act_hi_hot", "pool_hi_hot"))
        whose_ready, whose_turned, tanh_done = (s.sem(n) for n in ("whose_ready", "whose_turned", "tanh_done"))
        by_expert = lambda ap: ap.rearrange("p t e -> p e t")
        flat = lambda ap: ap.rearrange("p e t -> p (e t)")

        @block.sync
        def _(sp):
            if load:
                load(sp)

        @block.scalar
        def _(act):
            if capacity is None:
                nc.scalar.activation(tanh[:], core.tops[:], ACT.Tanh, scale=0.5).then_inc(tanh_done, 1)
            act.wait_ge(core.rank_loaded, 16 * 2)
            act.wait_ge(minus_hi_ready, 1)
            for a, g in enumerate(act_groups):
                if a >= 2:
                    act.wait_ge(act_hi_hot, a - 1)
                for u in range(per_group):
                    n = g * per_group + u
                    last = nc.scalar.activation(distance[a % 2][:, u, :], core.const16[:, P:P + tiles], ACT.Abs, bias=minus_hi[:, n:n + 1])
                last.then_inc(act_step, 1)
                act.wait_ge(act_step, a + 1)
                nc.scalar.activation(hi_hot[g][:], distance[a % 2][:], ACT.Relu, scale=-1.0, bias=1.0).then_inc(act_hi_hot, 1)

        @block.gpsimd
        def _(pool):
            pool.wait_ge(place_ready, 1)
            pool.tensor_tensor(picked[1][:], pick[1], place[:].rearrange("p e t -> p t e"), ALU.mult).then_inc(pool_picked, 1)
            pool.wait_ge(hi_ready, 1)
            pool.wait_ge(core.rank_loaded, 16 * 2)
            for g in pool_groups:
                for u in range(per_group):
                    n = g * per_group + u
                    last = pool.tensor_scalar(hi_hot[g][:, u, :], core.const16[:, P:P + tiles], hi[:, n:n + 1], None, ALU.is_equal)
                last.then_inc(pool_hi_hot, 1)

        @block.vector
        def _(vec):
            link = Linked(vec, vec_step)

            def hidden(n):
                vec.wait_ge(up_done, n + 1)
                nc.vector.tensor_tensor(hid[:, n, :], core.late_gate[:, n, :], up_ps[n % 2][:], ALU.mult).then_inc(hid_ready, 1)

            def update_x(k):
                vec.wait_ge(down_done, k + 1)
                xj = core.x[:, :, late[k], :]
                nc.vector.scalar_tensor_tensor(
                    xj, down_ps[:].rearrange("p (b d) -> p b d", d=D), 0.5, xj, ALU.mult, ALU.add
                ).then_inc(x_updated, 1)

            if load:
                nc.vector.memset(core.zero[:], 0.0)
                nc.vector.memset(core.ones_bf[:], 1.0)
                nc.vector.memset(core.ones16[:], 1.0)
            nc.vector.tensor_tensor(both[:], by_expert(pick[0]), by_expert(pick[1]), ALU.add).then_inc(both_ready, 1)
            if capacity is None:
                vec.wait_ge(tanh_done, 1)
                nc.vector.tensor_scalar(core.gates[:], tanh[:], 0.25, 0.25, ALU.mult, ALU.add)
            vec.wait_ge(core.rank_loaded, 16 * 2)
            vec.wait_ge(counted, 1)
            link(nc.vector.tensor_tensor_scan(
                flat(upto[:]), core.c("restart")[:, 0:cells], total_ps[:, 0:cells], 0.0, ALU.mult, ALU.add))
            link(nc.vector.tensor_tensor(flat(place[:]), flat(upto[:]), behind_ps[:, 0:cells], ALU.add))
            if capacity is None:
                link(nc.vector.tensor_scalar(rounded[:], upto[:, :, TILES - 1], float(P - 1), None, ALU.add))
                link(nc.vector.tensor_single_scalar(rounded[:], rounded[:], 7, ALU.arith_shift_right))
                link(nc.vector.tensor_copy(used_tiles[:], rounded[:]))
                link(nc.vector.tensor_tensor_scan(ends[:], core.c("ones")[:, 0:experts], used_tiles[:], 0.0, ALU.mult, ALU.add))
                link(nc.vector.tensor_tensor(base[:], ends[:], used_tiles[:], ALU.subtract))
                nc.vector.scalar_tensor_tensor(place[:], spread(base[:], TILES), float(P), place[:], ALU.mult, ALU.add).then_inc(place_ready, 1)
                vec.wait_ge(place_ready, 1)
                nc.vector.tensor_scalar(base[0:tiles, :], ends[0:tiles, :], core.c("part")[0:tiles, :], None,
                                        ALU.is_le, ALU.add, accum_out=whose[0:tiles, :]).then_inc(whose_ready, 1)
            else:
                link(nc.vector.tensor_scalar(work[:], place[:], float(capacity), FAR, ALU.is_ge, ALU.mult))
                link(nc.vector.tensor_tensor(place[:], place[:], work[:], ALU.add))
                nc.vector.tensor_tensor(place[:], place[:], spread(core.c("expert_base"), TILES), ALU.add).then_inc(place_ready, 1)
                vec.wait_ge(place_ready, 1)
            nc.vector.tensor_tensor(picked[0][:], pick[0], place[:].rearrange("p e t -> p t e"), ALU.mult).then_inc(picked_ready, 1)
            vec.wait_ge(picked_ready, 1)
            nc.vector.tensor_reduce(slot[:, 0, :], picked[0][:], axis=AX, op=ALU.add)
            vec.wait_ge(pool_picked, 1)
            link(nc.vector.tensor_reduce(slot[:, 1, :], picked[1][:], axis=AX, op=ALU.add))
            slots = slot[:].rearrange("p k t -> p (k t)")
            link(nc.vector.tensor_copy(slot_int[:], slots))
            link(nc.vector.tensor_single_scalar(hi_int[:], slot_int[:], 7, ALU.arith_shift_right))
            link(nc.vector.tensor_single_scalar(lo_int[:], slot_int[:], P - 1, ALU.bitwise_and))
            nc.vector.tensor_copy(hi[:], hi_int[:]).then_inc(hi_ready, 1)
            nc.vector.tensor_scalar(minus_hi[:], hi_int[:], -1.0, None, ALU.mult).then_inc(minus_hi_ready, 1)
            link(nc.vector.tensor_copy(lo[:], lo_int[:]))
            for g in range(groups):
                if g >= 2:
                    vec.wait_ge(hot_used, g - 1)
                for u in range(per_group):
                    n = g * per_group + u
                    last = nc.vector.tensor_scalar(
                        lo_hot[g % 2][:, u, :], core.const16[:, P:], lo[:, n:n + 1],
                        core.c("token_id")[:, n % TILES:n % TILES + 1], ALU.is_equal, ALU.mult)
                last.then_inc(lo_ready, 1)
                if g < 2 * len(late):
                    hidden(g)
                if 0 <= g - 3 and (g - 3) % 2 == 0 and (g - 3) // 2 < len(late):
                    update_x((g - 3) // 2)
            if capacity is None:
                nc.vector.tensor_copy(core.back_slot[:], slot[:])
                vec.wait_ge(whose_turned, 1)
                nc.vector.tensor_scalar(core.expert_ids[:], whose_ps[0:1, 0:tiles], float(experts - 1), None, ALU.min)
            else:
                link(nc.vector.tensor_scalar(clamped[:], slot[:], float(experts * capacity), None, ALU.min))
                nc.vector.tensor_copy(core.back_slot[:], clamped[:])
            vec.wait_ge(tokens_done, 1)
            nc.vector.tensor_scalar(core.gather_id[:, 0:tiles], token_ps[:, 0:tiles], float(ID_SHIFT), None, ALU.add)

        @block.tensor
        def _(pe):
            def up_of(n):
                j, h = halves[n]
                if n >= 2:
                    pe.wait_ge(hid_ready, n - 1)
                nc.tensor.matmul(up_ps[n % 2][:], core.shared_up[:, h * P:(h + 1) * P], core.norm_t[:, j, :],
                                 start=True, stop=True).then_inc(up_done, 1)

            pe.wait_ge(core.rank_loaded, 16 * 2)
            pe.wait_ge(both_ready, 1)
            nc.tensor.matmul(behind_ps[:, 0:cells], core.const16[:, 0:P], flat(both[:]), start=True, stop=True)
            nc.tensor.matmul(total_ps[:, 0:cells], core.ones16[:], flat(both[:]), start=True, stop=True).then_inc(counted, 1)
            if capacity is None:
                pe.wait_ge(whose_ready, 1)
                nc.tensor.matmul(whose_ps[0:1, 0:tiles], whose[0:tiles, :], core.c("ident")[0:tiles, 0:tiles],
                                 start=True, stop=True).then_inc(whose_turned, 1)
            if late:
                up_of(0)
                up_of(1)
            for g in range(groups):
                pe.wait_ge(lo_ready, g + 1)
                for of, ready in ((pool_groups, pool_hi_hot), (act_groups, act_hi_hot)):
                    if g in of:
                        pe.wait_ge(ready, of.index(g) + 1)
                for u in range(per_group):
                    n = g * per_group + u
                    last = nc.tensor.matmul(token_ps[:, 0:tiles], lo_hot[g % 2][:, u, :], hi_hot[g][:, u, :],
                                            start=(n == 0), stop=(n == choices - 1))
                last.then_inc(tokens_done if g == groups - 1 else hot_used, 1)
                if g + 2 < 2 * len(late):
                    up_of(g + 2)
                if g % 2 == 1 and g < 2 * len(late):
                    pe.wait_ge(hid_ready, g + 1)
                    if g >= 3:
                        pe.wait_ge(x_updated, g // 2)
                    shared_down_of(nc, core, hid[:, g - 1:g + 1, :], down_ps).then_inc(down_done, 1)



def ffn_experts(nc, core, tag, prepare=False):
    ring = 4
    width = lambda pair: min(2, FFN_TILES - 2 * pair)
    with Scope(nc, tag) as s, nc.Block() as block:
        rows = [s.sb(f"rows{k}", [P, 2, D]) for k in range(ring)]
        rows_t = [s.sb(f"rows_t{k}", [P, 2 * P]) for k in range(2)]
        gate = [s.sb(f"gate{k}", [P, 2, FFN_HID]) for k in range(2)]
        hid = [s.sb(f"hid{k}", [P, 2, FFN_HID]) for k in range(2)]
        hid_t = [s.sb(f"hid_t{k}", [P, 2 * P]) for k in range(2)]
        out = [s.sb(f"out{k}", [P, 2, D]) for k in range(2)]
        t_ps = [s.ps(f"t_ps{k}") for k in range(2)]
        gu_ps = [s.ps(f"gu_ps{k}", [P, 2, 2 * FFN_HID]) for k in range(2)]
        ht_ps = [s.ps(f"ht_ps{k}") for k in range(2)]
        out_ps = [s.ps(f"out_ps{k}") for k in range(2)]
        arrived = [s.sem(f"arrived{k}") for k in range(ring)]
        stored = [s.sem(f"stored{k}") for k in range(2)]
        turned, turn_copied, gu_done, silu_done, hid_ready = (
            s.sem(n) for n in ("turned", "turn_copied", "gu_done", "silu_done", "hid_ready"))
        hid_turned, hid_copied, out_done, out_copied = (
            s.sem(n) for n in ("hid_turned", "hid_copied", "out_done", "out_copied"))
        stores = core.ffn_out_rows.rearrange("(a p) d -> p a d", p=P)

        if prepare:
            rest = s.sb("rest", [1, BIAS_COLS])
            bias_parts = s.sb("bias_parts", [1, 3, BIAS_COLS], BF16)
            split_step, bias_split, bias_stored = s.sem("split_step"), s.sem("bias_split"), s.sem("bias_stored")


        @block.gpsimd
        def _(pool):
            for i in range(PAIRS):
                if i >= ring:
                    pool.wait_ge(turned, i - ring + 1)
                for h in range(width(i)):
                    tile = 2 * i + h
                    pool.indirect_dma_start(
                        out=rows[i % ring][:, h, :], out_offset=None, in_=core.norm_rows,
                        in_offset=bass.IndirectOffsetOnAxis(ap=core.gather_id[:, tile:tile + 1], axis=0),
                    ).then_inc(arrived[i % ring], 16)

        @block.tensor
        def _(pe):
            expert = {}
            pe.wait_ge(core.experts_loaded, 16 * 2)
            for i in range(PAIRS + 3):
                if i < PAIRS:
                    pe.wait_ge(arrived[i % ring], 32 * (i // ring) + 16 * width(i))
                    for h in range(width(i)):
                        last = nc.tensor.transpose(t_ps[i % 2][:, h * P:(h + 1) * P], rows[i % ring][:, h, :], core.c("ident"))
                    last.then_inc(turned, 1)
                q = i - 1
                if 0 <= q < PAIRS:
                    for h in range(width(q)):
                        expert[2 * q + h] = pe.value_load(
                            core.expert_ids[0:1, 2 * q + h:2 * q + h + 1], min_val=0, max_val=FFN_EXPERTS - 1)
                    pe.wait_ge(turn_copied, q + 1)
                    for h in range(width(q)):
                        last = nc.tensor.matmul(gu_ps[q % 2][:, h, :], rows_t[q % 2][:, h * P:(h + 1) * P],
                                                core.gate_up[:, expert[2 * q + h], :], start=True, stop=True)
                    last.then_inc(gu_done, 1)
                q = i - 2
                if 0 <= q < PAIRS:
                    pe.wait_ge(hid_ready, q + 1)
                    for h in range(width(q)):
                        last = nc.tensor.transpose(ht_ps[q % 2][:, h * P:(h + 1) * P], hid[q % 2][:, h, :], core.c("ident"))
                    last.then_inc(hid_turned, 1)
                q = i - 3
                if 0 <= q < PAIRS:
                    pe.wait_ge(hid_copied, q + 1)
                    if q >= 2:
                        pe.wait_ge(out_copied, q - 1)
                    for h in range(width(q)):
                        last = nc.tensor.matmul(out_ps[q % 2][:, h * P:(h + 1) * P], hid_t[q % 2][:, h * P:(h + 1) * P],
                                                core.down[:, expert.pop(2 * q + h), :], start=True, stop=True)
                    last.then_inc(out_done, 1)

        @block.scalar
        def _(act):
            for i in range(PAIRS + 3):
                if i < PAIRS:
                    act.wait_ge(turned, i + 1)
                    if i >= 2:
                        act.wait_ge(gu_done, i - 1)
                    nc.scalar.activation(rows_t[i % 2][:, 0:width(i) * P], t_ps[i % 2][:, 0:width(i) * P], ACT.Copy).then_inc(turn_copied, 1)
                q = i - 1
                if 0 <= q < PAIRS:
                    act.wait_ge(gu_done, q + 1)
                    if q >= 2:
                        act.wait_ge(hid_ready, q - 1)
                    nc.scalar.activation(gate[q % 2][:, 0:width(q), :], gu_ps[q % 2][:, 0:width(q), 0:FFN_HID], ACT.Silu).then_inc(silu_done, 1)
                q = i - 3
                if 0 <= q < PAIRS:
                    act.wait_ge(out_done, q + 1)
                    if q >= 2:
                        act.wait_ge(stored[q % 2], 16 * (q // 2))
                    nc.scalar.activation(out[q % 2][:, 0:width(q), :], out_ps[q % 2][:, 0:width(q) * P].rearrange("p (h d) -> p h d", d=D),
                                         ACT.Copy).then_inc(out_copied, 1)

        @block.vector
        def _(vec):
            if prepare:
                link = Linked(vec, split_step)
                vec.wait_ge(core.bias_loaded, 16 * 6)
                link(nc.vector.tensor_copy(bias_parts[:, 0, :], core.bias_row[:]))
                link(nc.vector.tensor_tensor(rest[:], core.bias_row[:], bias_parts[:, 0, :], ALU.subtract))
                link(nc.vector.tensor_copy(bias_parts[:, 1, :], rest[:]))
                link(nc.vector.tensor_tensor(rest[:], rest[:], bias_parts[:, 1, :], ALU.subtract))
                nc.vector.tensor_copy(bias_parts[:, 2, :], rest[:]).then_inc(bias_split, 1)
            for i in range(PAIRS + 2):
                q = i - 1
                if 0 <= q < PAIRS:
                    vec.wait_ge(silu_done, q + 1)
                    if q >= 2:
                        vec.wait_ge(hid_turned, q - 1)
                    nc.vector.tensor_tensor(hid[q % 2][:, 0:width(q), :], gate[q % 2][:, 0:width(q), :],
                                            gu_ps[q % 2][:, 0:width(q), FFN_HID:], ALU.mult).then_inc(hid_ready, 1)
                q = i - 2
                if 0 <= q < PAIRS:
                    vec.wait_ge(hid_turned, q + 1)
                    if q >= 2:
                        vec.wait_ge(out_done, q - 1)
                    nc.vector.tensor_copy(hid_t[q % 2][:, 0:width(q) * P], ht_ps[q % 2][:, 0:width(q) * P]).then_inc(hid_copied, 1)

        @block.sync
        def _(sp):
            if prepare:
                sp.wait_ge(bias_split, 1)
                for k in range(3):
                    sp.dma_start(core.bias3[k:k + 1, :], bias_parts[:, k, :]).then_inc(bias_stored, 16)
                sp.dma_start(core.moe_out_rows[MOE_ROWS:MOE_ROWS + P, :], core.zero[:]).then_inc(bias_stored, 16)
                sp.wait_ge(bias_stored, 16 * 4)
            for q in range(PAIRS):
                sp.wait_ge(out_copied, q + 1)
                sp.dma_start(stores[:, 2 * q:2 * q + width(q), :], out[q % 2][:, 0:width(q), :]).then_inc(stored[q % 2], 16)
            for k in range(2):
                sp.wait_ge(stored[k], 16 * (PAIRS // 2))



class Ring:

    def __init__(self, s, name, plan):
        self.banks = [s.ps(f"{name}{k}") for k in range(2)]
        self.filled = [s.sem(f"{name}_filled{k}") for k in range(2)]
        self.emptied = [s.sem(f"{name}_emptied{k}") for k in range(2)]
        self.at = {use: divmod(n, 2) for n, use in enumerate(plan)}

    def bank(self, *use):
        return self.banks[self.at[use][1]]

    def claim(self, pe, *use):
        turn, k = self.at[use]
        if turn:
            pe.wait_ge(self.emptied[k], turn)

    def fill(self, ins, *use):
        ins.then_inc(self.filled[self.at[use][1]], 1)

    def await_filled(self, eng, *use):
        turn, k = self.at[use]
        eng.wait_ge(self.filled[k], turn + 1)

    def empty(self, ins, *use):
        ins.then_inc(self.emptied[self.at[use][1]], 1)

    def await_emptied(self, eng, *use):
        turn, k = self.at[use]
        eng.wait_ge(self.emptied[k], turn + 1)


def attention(nc, core, tag, combine):
    S = SEQ_TILES
    first, end = -4, S + 6
    zcols = D + HEADS
    within = lambda j: 0 <= j < S

    def plan():
        for i in range(first, end):
            for what, j in (("q_t", i - 1), ("r1_t", i + 1), ("r2_t", i - 3), ("wo", i - 2), ("logits", i - 3), ("out_t", i - 1)):
                if within(j):
                    yield what, j

    with Scope(nc, tag) as s, nc.Block() as block:
        back = Returned(s, *combine)
        stats = s.sb("stats", [P, BATCH, 6])
        mean_var = [s.sb(f"mean_var{k}", [P, BATCH, 2]) for k in range(2)]
        neg_mean, var_eps, sd, rstd = (s.sb(n, [P, BATCH]) for n in ("neg_mean", "var_eps", "sd", "rstd"))
        unscale = [s.sb(f"unscale{k}", [P, BATCH]) for k in range(4)]
        rms1 = [s.sb(f"rms1{k}", [P, BATCH]) for k in range(2)]
        offset = [s.sb(f"offset{k}", [P, BATCH]) for k in range(2)]
        mean_sq2, rms2 = s.sb("mean_sq2", [P, BATCH]), s.sb("rms2", [P, BATCH])
        sum_sq = s.sb("sum_sq", [P, BATCH])
        r1 = [s.sb(f"r1_{k}", [P, BATCH, D]) for k in range(5)]
        r1_t = [s.sb(f"r1_t{k}", [P, BATCH * P]) for k in range(2)]
        turned_qk = s.sb("turned_qk", [P, BATCH, 2 * D])
        sin_part = s.sb("sin_part", [P, BATCH, 2 * D])
        exp_qk = s.sb("exp_qk", [P, BATCH, 2 * D])
        relu_qk = s.sb("relu_qk", [P, BATCH, 2 * D])
        phi = [s.sb(f"phi{k}", [P, BATCH, 2 * D]) for k in range(2)]
        v1 = [s.sb(f"v1_{k}", [P, BATCH, D + 1]) for k in range(2)]
        tanh = [s.sb(f"tanh{k}", [P, BATCH, D]) for k in range(2)]
        q_t = s.sb("q_t", [P, BATCH * P])
        state = [s.sb(f"state{c}", [P, BATCH, zcols]) for c in range(2)]
        den, recip = s.sb("den", [P, BATCH, HEADS]), s.sb("recip", [P, BATCH, HEADS])
        gated = s.sb("gated", [P, BATCH, D])
        heads = s.sb("heads", [P, BATCH, D])
        heads_t = s.sb("heads_t", [P, BATCH * P])
        square = s.sb("square", [P, BATCH, D])
        r2 = [s.sb(f"r2_{k}", [P, BATCH, D]) for k in range(2)]
        r2_t = s.sb("r2_t", [P, BATCH * P])

        probs = s.sb("probs", [P, BATCH, S, MOE_EXPERTS])
        same = s.sb("same", [P, BATCH, S, MOE_EXPERTS])
        most, total, inverse = (s.sb(n, [P, BATCH, S]) for n in ("most", "total", "inverse"))
        choice_parts = (slice(0, S - 2), slice(S - 2, S))
        by_step = lambda ap: ap.rearrange("p (b j) e -> p b j e", b=BATCH)
        tops = core.tops[:].rearrange("p k (b j) -> p k b j", b=BATCH)

        ring = Ring(s, "ring", plan())
        qk_ps, vg_ps = s.ps("qk_ps"), s.ps("vg_ps")
        kv_ps = s.ps("kv_ps", [P, 2, 512])
        num_ps = s.ps("num_ps", [P, 2, 512])

        names = ("stats_ready", "rstd_ready", "rms1_ready", "rms2_ready", "pool_step", "vec_step", "r1_ready",
                 "qk_done", "qk_read", "vg_done", "vg_read", "rope_ready", "act_done", "phi_ready",
                 "kv_done", "state_ready", "num_done", "num_read", "heads_ready", "sums_ready", "r2_ready",
                 "v_ones", "shifted", "exp_done")
        sig = {n: s.sem(n) for n in names}
        r2_stored = [s.sem(f"r2_stored{k}") for k in range(2)]
        rows = core.moe_rows.rearrange("(b j p) d -> j p b d", p=P, j=S)
        four = lambda ap: ap.rearrange("p (a c) n -> p a c n", c=2)
        kv = kv_ps[:, :, 0:2 * (D + 1)].rearrange("p a (c n) -> p a c n", n=D + 1)
        num = num_ps[:, :, 0:2 * zcols].rearrange("p a (c n) -> p a c n", n=zcols)

        @block.sync
        def _(sp):
            for j in range(S):
                sp.wait_ge(sig["r2_ready"], j + 1)
                sp.dma_start(rows[j], r2[j % 2][:]).then_inc(r2_stored[j % 2], 16)
            for k in range(2):
                sp.wait_ge(r2_stored[k], 16 * (S // 2))

        @block.gpsimd
        def _(pool):
            link = Linked(pool, sig["pool_step"])
            half = core.c("minus_half")
            for i in range(first, end):
                j = i - 3
                if within(j):
                    pool.wait_ge(sig["sums_ready"], j + 1)
                    link(pool.tensor_scalar(mean_sq2[:], sum_sq[:], 1.0 / D, None, ALU.mult))
                    if j >= 1:
                        pool.wait_ge(sig["r2_ready"], j)
                    pool.tensor_tensor(rms2[:], mean_sq2[:], half, ALU.pow).then_inc(sig["rms2_ready"], 1)
                j = i + 2
                if within(j):
                    back.gather_until(pool, 2 * BATCH * (j + 1) + ATTENTION_AHEAD[min(j, len(ATTENTION_AHEAD) - 1)])
                    pool.wait_ge(sig["stats_ready"], j + 1)
                    mean, var = mean_var[j % 2][:, :, 0], mean_var[j % 2][:, :, 1]
                    pool.tensor_scalar(neg_mean[:], mean, -1.0, None, ALU.mult)
                    pool.tensor_scalar(var_eps[:], var, LN_EPS, None, ALU.add)
                    if j >= 2:
                        pool.wait_ge(sig["r1_ready"], j - 1)
                    link(pool.tensor_tensor(rms1[j % 2][:], var, half, ALU.pow))
                    pool.tensor_tensor(offset[j % 2][:], neg_mean[:], rms1[j % 2][:], ALU.mult).then_inc(sig["rms1_ready"], 1)
                    link(pool.tensor_tensor(sd[:], var, rms1[j % 2][:], ALU.mult))
                    link(pool.tensor_tensor(rstd[:], var_eps[:], half, ALU.pow))
                    if j >= 4:
                        ring.await_emptied(pool, "wo", j - 4)
                    link(pool.tensor_tensor(unscale[j % 4][:], rstd[:], sd[:], ALU.mult))

        @block.scalar
        def _(act):
            def copy_out(dst, what, j, scale=None):
                ring.await_filled(act, what, j)
                if scale is None:
                    ins = nc.scalar.activation(dst, ring.bank(what, j)[:], ACT.Copy)
                else:
                    ins = nc.scalar.activation(dst, ring.bank(what, j)[:], ACT.Copy, scale=scale)
                ring.empty(ins, what, j)

            act.wait_ge(core.attention_loaded, 16 * 9)

            def exp_logits(k):
                act.wait_ge(sig["shifted"], k + 1)
                here = choice_parts[k]
                nc.scalar.activation(probs[:, :, here, :], by_step(core.logits[:])[:, :, here, :], ACT.Exp).then_inc(sig["exp_done"], 1)

            def values_gates(j, q):
                act.wait_ge(sig["vg_done"], 2 * j + q + 1)
                if j >= 2 and q == 0:
                    act.wait_ge(sig["kv_done"], 2 * (j - 1))
                    act.wait_ge(sig["heads_ready"], j - 1)
                if j == 0 and q == 0:
                    act.wait_ge(sig["v_ones"], 1)
                vg = vg_ps[:].rearrange("p (t n) -> p t n", t=2)
                nc.scalar.activation(v1[j % 2][:, 2 * q:2 * q + 2, 0:D], vg[:, :, 0:D], ACT.Copy)
                nc.scalar.activation(tanh[j % 2][:, 2 * q:2 * q + 2, :], vg[:, :, D:], ACT.Tanh, scale=0.5
                                     ).then_inc(sig["vg_read"], 1)

            for i in range(first, end):
                if within(i):
                    values_gates(i, 1)
                if within(i):
                    act.wait_ge(sig["rope_ready"], i + 1)
                    if i >= 1:
                        act.wait_ge(sig["phi_ready"], i)
                    nc.scalar.activation(exp_qk[:], turned_qk[:], ACT.Exp)
                    nc.scalar.activation(relu_qk[:], turned_qk[:], ACT.Relu).then_inc(sig["act_done"], 1)
                j = i - 2
                if within(j):
                    ring.await_emptied(act, "wo", j)
                    if j >= 1:
                        act.wait_ge(sig["rms2_ready"], j)
                    for b in range(BATCH):
                        last = nc.scalar.activation(square[:, b, :], core.a1[:, b, j, :], ACT.Square, accum_out=sum_sq[:, b:b + 1])
                    last.then_inc(sig["sums_ready"], 1)
                j = i + 2
                if within(j):
                    act.wait_ge(sig["rms1_ready"], j + 1)
                    if j >= 5:
                        ring.await_emptied(act, "wo", j - 5)
                    for b in range(BATCH):
                        last = nc.scalar.activation(r1[j % 5][:, b, :], core.x[:, b, j, :], ACT.Identity,
                                                    bias=offset[j % 2][:, b:b + 1], scale=rms1[j % 2][:, b:b + 1])
                    last.then_inc(sig["r1_ready"], 1)
                j = i - 2
                if within(j):
                    act.wait_ge(sig["rms2_ready"], j + 1)
                    if j >= 2:
                        ring.await_filled(act, "r2_t", j - 2)
                        act.wait_ge(r2_stored[j % 2], 16 * (j // 2))
                    for b in range(BATCH):
                        last = nc.scalar.activation(r2[j % 2][:, b, :], core.a1[:, b, j, :], ACT.Copy, scale=rms2[:, b:b + 1])
                    last.then_inc(sig["r2_ready"], 1)
                if within(i - 1):
                    if i - 1 >= 1:
                        ring.await_filled(act, "wo", i - 2)
                    copy_out(heads_t[:], "out_t", i - 1)
                if within(i + 1):
                    values_gates(i + 1, 0)
                if within(i):
                    if i >= 1:
                        act.wait_ge(sig["num_done"], 2 * i)
                    copy_out(q_t[:], "q_t", i)
                if within(i + 2):
                    if i + 2 >= 2:
                        act.wait_ge(sig["vg_done"], 2 * (i + 1))
                    copy_out(r1_t[(i + 2) % 2][:], "r1_t", i + 2, core.norm1[:])
                if within(i - 2):
                    if i - 2 >= 1:
                        ring.await_filled(act, "logits", i - 3)
                    copy_out(r2_t[:], "r2_t", i - 2, core.norm2[:])
                    if i - 2 == S - 2:
                        exp_logits(0)

            exp_logits(1)

        @block.vector
        def _(vec):
            link = Linked(vec, sig["vec_step"])
            vec.wait_ge(core.attention_loaded, 16 * 9)
            for k in range(2):
                last = nc.vector.memset(v1[k][:, :, D:D + 1], 1.0)
            last.then_inc(sig["v_ones"], 1)
            cos_of = lambda i: spread(core.c("cos")[:, i * DK:(i + 1) * DK], 4 * HEADS, inner=False)
            sin_of = lambda i: spread(core.c("sin")[:, i * DK:(i + 1) * DK], 4 * HEADS, inner=False)

            def rotary(i, q):
                vec.wait_ge(sig["qk_done"], 2 * i + q + 1)
                if i >= 1 and q == 0:
                    vec.wait_ge(sig["act_done"], i)
                two = lambda x: x[:, 2 * q:2 * q + 2, :].rearrange("p t (h d) -> p (t h) d", d=DK)
                by_head = qk_ps[:].rearrange("p (h d) -> p h d", d=DK)
                nc.vector.tensor_tensor(two(turned_qk), by_head, cos_of(i), ALU.mult)
                nc.vector.tensor_tensor(two(sin_part), by_head, sin_of(i), ALU.mult).then_inc(sig["qk_read"], 1)

            def shift_logits(k):
                here = choice_parts[k]
                logits = by_step(core.logits[:])[:, :, here, :]
                shape = list(logits.shape)
                link(nc.vector.tensor_reduce(most[:, :, here], logits, axis=AX, op=ALU.max))
                nc.vector.tensor_tensor(logits, logits, most[:, :, here].unsqueeze(3).to_broadcast(shape), ALU.subtract
                                        ).then_inc(sig["shifted"], 1)

            def choose(k):
                here = choice_parts[k]
                part = probs[:, :, here, :]
                sums, inv = total[:, :, here], inverse[:, :, here]
                vec.wait_ge(sig["exp_done"], k + 1)
                link(nc.vector.tensor_reduce(sums, part, axis=AX, op=ALU.add))
                link(nc.vector.reciprocal(inv, sums))
                link(nc.vector.tensor_tensor(part, part, inv.unsqueeze(3).to_broadcast(list(part.shape)), ALU.mult))
                top_two(nc, link, part, core.c("rev")[:, 0:MOE_EXPERTS],
                        [by_step(core.moe_pick[q])[:, :, here, :] for q in range(2)],
                        [tops[:, q, :, here] for q in range(2)], (same[:, :, here, :], most[:, :, here]))
                link(nc.vector.tensor_tensor(sums, tops[:, 0, :, here], tops[:, 1, :, here], ALU.add))
                link(nc.vector.reciprocal(inv, sums))
                for q in range(2):
                    nc.vector.tensor_tensor(core.moe_gates[:].rearrange("p k (b j) -> p k b j", b=BATCH)[:, q, :, here],
                                            tops[:, q, :, here], inv, ALU.mult)

            def state_after(j, c):
                vec.wait_ge(sig["kv_done"], 2 * j + c + 1)
                if j >= 1:
                    vec.wait_ge(sig["num_done"], 2 * (j - 1) + c + 1)
                mask = core.c("headmask").unsqueeze(1).unsqueeze(1).to_broadcast([P, 2, 2, D])
                nc.vector.tensor_tensor(four(state[c][:, :, 0:D]), kv[:, :, :, 0:D], mask, ALU.mult)
                col = core.c("headcol").unsqueeze(1).unsqueeze(1).to_broadcast([P, 2, 2, HEADS])
                nc.vector.tensor_tensor(four(state[c][:, :, D:]), kv[:, :, :, D:D + 1].to_broadcast([P, 2, 2, HEADS]), col, ALU.mult
                                        ).then_inc(sig["state_ready"], 1)

            for i in range(first, end):
                if within(i):
                    rotary(i, 1)
                if within(i):
                    vec.wait_ge(sig["qk_read"], 2 * i + 2)
                    split = lambda x: x[:].rearrange("p t (h s d) -> p (t h) s d", s=2, d=DK // 2)
                    nc.vector.tensor_tensor(split(turned_qk)[:, :, 0, :], split(turned_qk)[:, :, 0, :], split(sin_part)[:, :, 1, :], ALU.add)
                    nc.vector.tensor_tensor(split(turned_qk)[:, :, 1, :], split(turned_qk)[:, :, 1, :], split(sin_part)[:, :, 0, :], ALU.add
                                            ).then_inc(sig["rope_ready"], 1)
                if within(i - 1):
                    state_after(i - 1, 1)
                j = i - 2
                if within(j):
                    ring.await_filled(vec, "wo", j)
                    for b in range(BATCH):
                        ins = nc.vector.scalar_tensor_tensor(core.a1[:, b, j, :], r1[j % 5][:, b, :], unscale[j % 4][:, b:b + 1],
                                                             ring.bank("wo", j)[:, b * D:(b + 1) * D], ALU.mult, ALU.add)
                    ring.empty(ins, "wo", j)
                j = i - 1
                if within(j):
                    vec.wait_ge(sig["num_done"], 2 * j + 2)
                    link(nc.vector.tensor_scalar(four(den[:]), num[:, :, :, D:], 2.0, 2.0 * DEN_EPS, ALU.mult, ALU.add))
                    nc.vector.reciprocal(recip[:], den[:])
                    for a in range(2):
                        last = nc.vector.scalar_tensor_tensor(
                            gated[:, 2 * a:2 * a + 2, :], tanh[j % 2][:, 2 * a:2 * a + 2, :], 1.0, num[:, a, :, 0:D], ALU.add, ALU.mult)
                    last.then_inc(sig["num_read"], 1)
                    vec.wait_ge(sig["num_read"], j + 1)
                    if j >= 1:
                        ring.await_filled(vec, "out_t", j - 1)
                    by_head = lambda ap: ap.rearrange("p b (h d) -> p (b h) d", d=DK)
                    nc.vector.tensor_tensor(by_head(heads[:]), by_head(gated[:]),
                                            recip[:].rearrange("p b h -> p (b h)").unsqueeze(2).to_broadcast([P, BATCH * HEADS, DK]), ALU.mult
                                            ).then_inc(sig["heads_ready"], 1)
                if within(i):
                    vec.wait_ge(sig["act_done"], i + 1)
                    if i >= 2:
                        vec.wait_ge(sig["kv_done"], 2 * (i - 1))
                    nc.vector.scalar_tensor_tensor(phi[i % 2][:], exp_qk[:], 1.0, relu_qk[:], ALU.min, ALU.add
                                                   ).then_inc(sig["phi_ready"], 1)
                j = i - 3
                if within(j):
                    ring.await_filled(vec, "logits", j)
                    ins = nc.vector.tensor_tensor(
                        core.logits[:, j:TILES:S, :], ring.bank("logits", j)[:, 0:BATCH * MOE_EXPERTS].rearrange("p (b e) -> p b e", b=BATCH),
                        spread(core.router_bias[:], BATCH, inner=False), ALU.add)
                    ring.empty(ins, "logits", j)
                    if j == S - 3:
                        ring.await_emptied(vec, "logits", j)
                        shift_logits(0)
                    if j == S - 2:
                        choose(0)
                    if j == S - 1:
                        ring.await_emptied(vec, "logits", j)
                        shift_logits(1)
                        choose(1)
                if within(i + 1):
                    rotary(i + 1, 0)
                if within(i + 3):
                    back.add(nc, vec, core.x[:, :, i + 3, :], i + 3)
                if within(i):
                    state_after(i, 0)
                if within(i + 3):
                    statistics(nc, link, vec, core.x[:, :, i + 3, :], stats, mean_var[(i + 1) % 2], sig["stats_ready"])

        @block.tensor
        def _(pe):
            ones3 = core.ones_bf[0:3, :]
            pe.wait_ge(core.attention_loaded, 16 * 9)

            def turn(what, j, src):
                ring.claim(pe, what, j)
                for b in range(BATCH):
                    last = nc.tensor.transpose(ring.bank(what, j)[:, b * P:(b + 1) * P], src(b), core.c("ident"))
                ring.fill(last, what, j)

            def bias(out, at, width, times):
                nc.tensor.matmul(out, ones3, core.bias3[:, at:at + width].unsqueeze(1).to_broadcast([3, times, width]),
                                 start=True, stop=False, skip_group_check=True)

            def states(j, c):
                if c == 0:
                    pe.wait_ge(sig["phi_ready"], j + 1)
                    pe.wait_ge(sig["vg_read"], 2 * j + 2)
                if 2 * j + c >= 1:
                    pe.wait_ge(sig["state_ready"], 2 * j + c)
                rows_c = slice(c * CHUNK, (c + 1) * CHUNK)
                for b in range(BATCH):
                    last = nc.tensor.matmul(kv[:, b // 2, b % 2, :], phi[j % 2][rows_c, b, D:], v1[j % 2][rows_c, b, :],
                                            start=(j == 0 and c == 0 and b % 2 == 0), stop=True, skip_group_check=True)
                last.then_inc(sig["kv_done"], 1)

            def numerators(j, c):
                pe.wait_ge(sig["state_ready"], 2 * j + c + 1)
                ring.await_emptied(pe, "q_t", j)
                if j >= 1:
                    pe.wait_ge(sig["num_read"], j)
                rows_c = slice(c * CHUNK, (c + 1) * CHUNK)
                for b in range(BATCH):
                    last = nc.tensor.matmul(num[rows_c, b // 2, b % 2, :], q_t[:, b * P + c * CHUNK:b * P + (c + 1) * CHUNK],
                                            state[c][:, b, :], start=True, stop=True, skip_group_check=True)
                last.then_inc(sig["num_done"], 1)

            def project(j, q, bank, at, done, read):
                ring.await_emptied(pe, "r1_t", j)
                if 2 * j + q >= 1:
                    pe.wait_ge(read, 2 * j + q)
                bias(bank[:].rearrange("p (t n) -> p t n", t=2), at, 2 * D, 2)
                for t in range(2):
                    b = 2 * q + t
                    last = nc.tensor.matmul(bank[:, t * 2 * D:(t + 1) * 2 * D], r1_t[j % 2][:, b * P:(b + 1) * P],
                                            core.qkvg[:].rearrange("c k n -> c (k n)")[:, at:at + 2 * D],
                                            start=False, stop=(t == 1), skip_group_check=True)
                last.then_inc(done, 1)

            def project_qk(j, q):
                project(j, q, qk_ps, 0, sig["qk_done"], sig["qk_read"])

            def project_vg(j, q):
                project(j, q, vg_ps, 2 * D, sig["vg_done"], sig["vg_read"])

            for i in range(first, end):
                if within(i - 1):
                    pe.wait_ge(sig["phi_ready"], i)
                    turn("q_t", i - 1, lambda b: phi[(i - 1) % 2][:, b, 0:D])
                if within(i):
                    project_qk(i, 1)
                if within(i):
                    project_vg(i, 1)
                if within(i - 1):
                    numerators(i - 1, 0)
                if within(i + 1):
                    pe.wait_ge(sig["r1_ready"], i + 2)
                    turn("r1_t", i + 1, lambda b: r1[(i + 1) % 5][:, b, :])
                if within(i - 3):
                    pe.wait_ge(sig["r2_ready"], i - 2)
                    turn("r2_t", i - 3, lambda b: r2[(i - 3) % 2][:, b, :])
                if within(i - 1):
                    states(i - 1, 1)
                if within(i - 2):
                    ring.await_emptied(pe, "out_t", i - 2)
                    ring.claim(pe, "wo", i - 2)
                    bank = ring.bank("wo", i - 2)
                    bias(bank[:].rearrange("p (t n) -> p t n", t=BATCH), 4 * D, D, BATCH)
                    for b in range(BATCH):
                        last = nc.tensor.matmul(bank[:, b * D:(b + 1) * D], heads_t[:, b * P:(b + 1) * P], core.wo[:],
                                                start=False, stop=(b == BATCH - 1), skip_group_check=True)
                    ring.fill(last, "wo", i - 2)
                if within(i - 1):
                    numerators(i - 1, 1)
                if within(i + 1):
                    project_qk(i + 1, 0)
                if within(i - 3):
                    ring.await_emptied(pe, "r2_t", i - 3)
                    ring.claim(pe, "logits", i - 3)
                    for b in range(BATCH):
                        last = nc.tensor.matmul(ring.bank("logits", i - 3)[:, b * MOE_EXPERTS:(b + 1) * MOE_EXPERTS],
                                                r2_t[:, b * P:(b + 1) * P], core.moe_router[:], start=True, stop=True)
                    ring.fill(last, "logits", i - 3)
                if within(i + 1):
                    project_vg(i + 1, 0)
                if within(i - 1):
                    pe.wait_ge(sig["heads_ready"], i)
                    turn("out_t", i - 1, lambda b: heads[:, b, :])
                if within(i):
                    pe.wait_ge(sig["phi_ready"], i + 1)
                    states(i, 0)



def moe_experts(nc, core, tag):
    half = CAPACITY // 2
    assert MOE_EXPERTS == SEQ_TILES
    split = 3
    parts = ((0, split), (split, CAP_TILES))
    with Scope(nc, tag) as s, nc.Block() as block:
        rows = [s.sb(f"rows{k}", [P, CAP_TILES, D]) for k in range(2)]
        rows_t = [s.sb(f"rows_t{k}", [P, CAPACITY]) for k in range(2)]
        hid = [s.sb(f"hid{k}", [P, HID_CHUNKS, CAPACITY]) for k in range(2)]
        out = [s.sb(f"out{k}", [P, CAP_TILES, D]) for k in range(2)]
        t_ps = [s.ps(f"t_ps{k}") for k in range(2)]
        hid_ps = [s.ps(f"hid_ps{k}") for k in range(4)]
        out_ps = [s.ps(f"out_ps{k}") for k in range(2)]
        arrived = [[s.sem(f"arrived{k}_{part}") for part in range(2)] for k in range(2)]
        stored = [s.sem(f"stored{k}") for k in range(2)]
        turned, turn_copied, hid_done, gelu_done, out_done, out_copied = (
            s.sem(n) for n in ("turned", "turn_copied", "hid_done", "gelu_done", "out_done", "out_copied"))
        stores = core.moe_out_rows[0:MOE_ROWS, :].rearrange("(e t p) d -> e p t d", p=P, t=CAP_TILES)
        units = [(c, h) for h in range(2) for c in range(HID_CHUNKS)]
        assert half <= split * P

        @block.gpsimd
        def _(pool):
            for e in range(MOE_EXPERTS):
                if e >= 2:
                    pool.wait_ge(turned, 2 * (e - 1))
                for t in range(CAP_TILES):
                    n = e * CAP_TILES + t
                    pool.indirect_dma_start(
                        out=rows[e % 2][:, t, :], out_offset=None, in_=core.moe_rows,
                        in_offset=bass.IndirectOffsetOnAxis(ap=core.gather_id[:, n:n + 1], axis=0),
                    ).then_inc(arrived[e % 2][int(t >= split)], 16)

        @block.tensor
        def _(pe):
            def turn(e):
                for k, (lo, hi) in enumerate(parts):
                    pe.wait_ge(arrived[e % 2][k], 16 * (hi - lo) * (e // 2 + 1))
                    if e >= 1:
                        pe.wait_ge(turn_copied, 2 * (e - 1) + k + 1)
                    for t in range(lo, hi):
                        last = nc.tensor.transpose(t_ps[k][:, (t - lo) * P:(t - lo + 1) * P], rows[e % 2][:, t, :], core.c("ident"))
                    last.then_inc(turned, 1)

            pe.wait_ge(core.moe_loaded, 16 * (1 + 2 * MOE_EXPERTS))
            turn(0)
            for e in range(MOE_EXPERTS):
                for u, (c, h) in enumerate(units):
                    n = len(units) * e + u
                    pe.wait_ge(turn_copied, 2 * e + h + 1)
                    if n >= 4:
                        pe.wait_ge(gelu_done, n - 3)
                    nc.tensor.matmul(hid_ps[n % 4][:, 0:half], core.w1[:, e, c * P:(c + 1) * P],
                                     rows_t[e % 2][:, h * half:(h + 1) * half], start=True, stop=True).then_inc(hid_done, 1)
                if e + 1 < MOE_EXPERTS:
                    turn(e + 1)
                pe.wait_ge(gelu_done, len(units) * (e + 1))
                for k, (lo, hi) in enumerate(parts):
                    if e >= 1:
                        pe.wait_ge(out_copied, 2 * (e - 1) + k + 1)
                    for t in range(lo, hi):
                        dst = out_ps[k][:, (t - lo) * D:(t - lo + 1) * D]
                        nc.tensor.matmul(dst, core.ones_bf[0:3, :], core.bias3[:, 5 * D + e * D:5 * D + (e + 1) * D], start=True, stop=False)
                        for c in range(HID_CHUNKS):
                            last = nc.tensor.matmul(dst, hid[e % 2][:, c, t * P:(t + 1) * P], core.w2[:, e, c, :],
                                                    start=False, stop=(c == HID_CHUNKS - 1))
                    last.then_inc(out_done, 1)

        @block.scalar
        def _(act):
            act.wait_ge(core.moe_loaded, 16 * (1 + 2 * MOE_EXPERTS))
            for e in range(MOE_EXPERTS):
                for u, (c, h) in enumerate(units):
                    n = len(units) * e + u
                    act.wait_ge(hid_done, n + 1)
                    if u == 0 and e >= 2:
                        act.wait_ge(out_done, 2 * (e - 1))
                    bias = e * HID_CHUNKS + c
                    nc.scalar.activation(hid[e % 2][:, c, h * half:(h + 1) * half], hid_ps[n % 4][:, 0:half], ACT.Gelu,
                                         bias=core.b1[:, bias:bias + 1]).then_inc(gelu_done, 1)

        @block.vector
        def _(vec):
            def copy_turned(e):
                for k, (lo, hi) in enumerate(parts):
                    vec.wait_ge(turned, 2 * e + k + 1)
                    if e >= 2 and k == 0:
                        vec.wait_ge(hid_done, len(units) * (e - 1))
                    nc.vector.tensor_scalar(rows_t[e % 2][:, lo * P:hi * P], t_ps[k][:, 0:(hi - lo) * P], core.norm2[:], None, ALU.mult
                                            ).then_inc(turn_copied, 1)

            copy_turned(0)
            for e in range(MOE_EXPERTS):
                nc.vector.tensor_tensor(core.x[:, :, e, :], core.x[:, :, e, :], core.a1[:, :, e, :], ALU.add)
                if e + 1 < MOE_EXPERTS:
                    copy_turned(e + 1)
                for k, (lo, hi) in enumerate(parts):
                    vec.wait_ge(out_done, 2 * e + k + 1)
                    if k == 0 and e >= 2:
                        vec.wait_ge(stored[e % 2], 16 * (e // 2))
                    nc.vector.tensor_copy(out[e % 2][:, lo:hi, :], out_ps[k][:, 0:(hi - lo) * D].rearrange("p (t d) -> p t d", d=D)
                                          ).then_inc(out_copied, 1)

        @block.sync
        def _(sp):
            for e in range(MOE_EXPERTS):
                sp.wait_ge(out_copied, 2 * e + 2)
                sp.dma_start(stores[e], out[e % 2][:]).then_inc(stored[e % 2], 16)
            for k in range(2):
                sp.wait_ge(stored[k], 16 * (MOE_EXPERTS // 2))


def ffn_last(nc, core, tag, combine, out):
    out_steps = out.rearrange("b (j p) d -> j p b d", p=P)
    with Scope(nc, tag) as s, nc.Block() as block:
        back = Returned(s, *combine)
        gate = s.sb("gate", [P, 2, BATCH * P])
        hid = [s.sb(f"hid{k}", [P, 2, BATCH * P]) for k in range(2)]
        gate_ps = [s.ps(f"gate_ps{k}") for k in range(2)]
        up_ps = [s.ps(f"up_ps{k}") for k in range(2)]
        down_ps = [s.ps(f"down_ps{k}") for k in range(2)]
        gate_done, up_done, silu_done, hid_ready, down_done, shared_added = (
            s.sem(n) for n in ("gate_done", "up_done", "silu_done", "hid_ready", "down_done", "shared_added"))
        out_stored = core.out_stored

        @block.gpsimd
        def _(pool):
            back.gather_until(pool, 2 * BATCH * SEQ_TILES)

        @block.scalar
        def _(act):
            for j in range(SEQ_TILES):
                for h in range(2):
                    act.wait_ge(gate_done, 2 * j + h + 1)
                    if j >= 1:
                        act.wait_ge(hid_ready, 2 * (j - 1) + h + 1)
                    nc.scalar.activation(gate[:, h, :], gate_ps[h][:], ACT.Silu).then_inc(silu_done, 1)

        @block.vector
        def _(vec):
            def hidden(j):
                for h in range(2):
                    vec.wait_ge(silu_done, 2 * j + h + 1)
                    vec.wait_ge(up_done, 2 * j + h + 1)
                    if h == 0 and j >= 2:
                        vec.wait_ge(down_done, j - 1)
                    nc.vector.tensor_tensor(hid[j % 2][:, h, :], gate[:, h, :], up_ps[h][:], ALU.mult).then_inc(hid_ready, 1)

            hidden(0)
            for j in range(SEQ_TILES):
                if j + 1 < SEQ_TILES:
                    hidden(j + 1)
                xj = core.x[:, :, j, :]
                vec.wait_ge(down_done, j + 1)
                nc.vector.scalar_tensor_tensor(
                    xj, down_ps[j % 2][:].rearrange("p (b d) -> p b d", d=D), 0.5, xj, ALU.mult, ALU.add
                ).then_inc(shared_added, 1)
                vec.wait_ge(shared_added, j + 1)
                back.add(nc, vec, xj, j)

        @block.tensor
        def _(pe):
            for i in range(SEQ_TILES + 1):
                for h in range(2 if i < SEQ_TILES else 0):
                    if i >= 1:
                        pe.wait_ge(silu_done, 2 * (i - 1) + h + 1)
                    nc.tensor.matmul(gate_ps[h][:], core.shared_gate[:, h * P:(h + 1) * P], core.norm_t[:, i, :],
                                     start=True, stop=True).then_inc(gate_done, 1)
                    if i >= 1:
                        pe.wait_ge(hid_ready, 2 * (i - 1) + h + 1)
                    nc.tensor.matmul(up_ps[h][:], core.shared_up[:, h * P:(h + 1) * P], core.norm_t[:, i, :],
                                     start=True, stop=True).then_inc(up_done, 1)
                q = i - 1
                if q >= 0:
                    pe.wait_ge(hid_ready, 2 * q + 2)
                    if q >= 2:
                        pe.wait_ge(shared_added, q - 1)
                    shared_down_of(nc, core, hid[q % 2], down_ps[q % 2]).then_inc(down_done, 1)

        @block.sync
        def _(sp):
            for j in range(SEQ_TILES):
                sp.wait_ge(back.used, j + 1)
                sp.dma_start(out_steps[j], core.x[:, :, j, :]).then_inc(out_stored, 16)
            sp.wait_ge(out_stored, 16 * SEQ_TILES)



def allocate(nc, stack):
    core = Core()

    def sb(name, shape, dt=F32):
        return stack.enter_context(nc.sbuf_tensor(f"core_{name}", shape, dt))

    core.x = sb("x", [P, BATCH, SEQ_TILES, D])
    core.a1 = sb("a1", [P, BATCH, SEQ_TILES, D])
    core.norm_t = core.a1[:].rearrange("p b j d -> p (b j d)").rearrange("p (j n) -> p j n", j=SEQ_TILES)
    core.const = sb("const", [P, CONST_COLS])
    core.gate_up = sb("gate_up", [P, FFN_EXPERTS, 2 * FFN_HID])
    core.down = sb("down", [P, FFN_EXPERTS, D])
    core.ffn_router = sb("ffn_router", [P, FFN_EXPERTS])
    core.shared_gate = sb("shared_gate", [P, SHARED])
    core.shared_up = sb("shared_up", [P, SHARED])
    core.shared_down = sb("shared_down", [P, 2, D])
    core.qkvg = sb("qkvg", [P, 4, D])
    core.wo = sb("wo", [P, D])
    core.norm1 = sb("norm1", [P, 1])
    core.norm2 = sb("norm2", [P, 1])
    core.moe_router = sb("moe_router", [P, MOE_EXPERTS])
    core.router_bias = sb("router_bias", [P, MOE_EXPERTS])
    core.b1 = sb("b1", [P, MOE_EXPERTS * HID_CHUNKS])
    core.w1 = sb("w1", [P, MOE_EXPERTS, MOE_HID])
    core.w2 = sb("w2", [P, MOE_EXPERTS, HID_CHUNKS, D])
    core.bias_row = sb("bias_row", [1, BIAS_COLS])
    core.bias3 = sb("bias3", [3, BIAS_COLS], BF16)
    core.const16 = sb("const16", [P, 2 * P], F16)
    core.zero = sb("zero", [P, D])
    core.ones16 = sb("ones16", [P, P], F16)
    core.ones_bf = sb("ones_bf", [3, P], BF16)
    core.pick_all = stack.enter_context(nc.sbuf_tensor("core_pick", [P, 2, TILES * FFN_EXPERTS], F32))
    core.late_gate = sb("late_gate", [P, 2 * LATE, BATCH * P])
    core.tops = sb("tops", [P, 2, TILES])
    core.logits = sb("logits", [P, TILES, MOE_EXPERTS])
    core.gates = sb("gates", [P, 2, TILES])
    core.moe_gates = sb("moe_gates", [P, 2, TILES])
    core.back_slot = sb("back_slot", [P, 2, TILES], I32)
    core.gather_id = sb("gather_id", [P, 2 * PAIRS], I32)
    core.expert_ids = sb("expert_ids", [1, 2 * PAIRS], I32)
    core.pick = [core.pick_all[:, k, :].rearrange("p (t e) -> p t e", e=FFN_EXPERTS) for k in range(2)]
    core.moe_pick = [core.pick_all[:, k, 0:TILES * MOE_EXPERTS].rearrange("p (t e) -> p t e", e=MOE_EXPERTS) for k in range(2)]
    core.c = lambda name: core.const[:, CONST_AT[name][0]:CONST_AT[name][1]]
    core.norm_rows = nc.dram_tensor("norm_rows", [TOKENS, D], F32, kind="Internal").ap()
    core.ffn_out_rows = nc.dram_tensor("ffn_out_rows", [FFN_TILES * P, D], F32, kind="Internal").ap()
    core.moe_rows = nc.dram_tensor("moe_rows", [TOKENS, D], F32, kind="Internal").ap()
    core.moe_out_rows = nc.dram_tensor("moe_out_rows", [MOE_ROWS + P, D], F32, kind="Internal").ap()
    return core


def add_semaphores(nc, core, stack):
    sem = lambda name: stack.enter_context(nc.semaphore(f"core_{name}"))
    core.x_loaded = [sem(f"x_loaded{j}") for j in range(SEQ_TILES)]
    core.const_loaded, core.shared_loaded, core.rank_loaded = sem("const_loaded"), sem("shared_loaded"), sem("rank_loaded")
    core.experts_loaded, core.bias_loaded = sem("experts_loaded"), sem("bias_loaded")
    core.attention_loaded, core.moe_loaded = sem("attention_loaded"), sem("moe_loaded")
    core.out_stored = sem("out_stored")


def build(nc, w, x, out):
    Scope.sems = []
    with ExitStack() as stack:
        core = allocate(nc, stack)
        add_semaphores(nc, core, stack)
        ffn_back = (core.ffn_out_rows, core.back_slot, core.gates)
        moe_back = (core.moe_out_rows, core.back_slot, core.moe_gates)
        ffn_front(nc, core, "front1", load=lambda sp: load_first(sp, core, w, x))
        rank(nc, core, "rank1", core.pick, FFN_EXPERTS, 2 * PAIRS, load=lambda sp: load_rest(sp, core, w),
             late=range(SEQ_TILES - LATE, SEQ_TILES))
        ffn_experts(nc, core, "ffn1", prepare=True)
        free_semaphores(nc)
        attention(nc, core, "attn", ffn_back)
        rank(nc, core, "rank2", core.moe_pick, MOE_EXPERTS, MOE_TILES, CAPACITY)
        moe_experts(nc, core, "moe")
        ffn_front(nc, core, "front3", moe_back)
        rank(nc, core, "rank3", core.pick, FFN_EXPERTS, 2 * PAIRS)
        ffn_experts(nc, core, "ffn3")
        ffn_last(nc, core, "last", ffn_back, out)


PLAIN = dict(
    wq="Wq", wk="Wk", wv="Wv", wg="Wg", wo="Wo", bq="bq", bk="bk", bv="bv", bg="bg", bo="bo",
    norm1="norm1_scale", norm2="norm2_scale", moe_router="router_W", router_bias="router_b",
    w1="W1", b1="b1", w2="W2", b2="b2",
)
FFN_PLAIN = dict(gate_up="gate_up_w", down="down_w")
FFN_TURNED = dict(ffn_router="router_w", shared_gate="shared_gate_w", shared_up="shared_up_w", shared_down="shared_down_w")


def host_arrays(inputs):
    arrays = {"x": np.ascontiguousarray(inputs["L0_attn_x"]), "const": constants(), "const16": constants16()}
    for name, given in PLAIN.items():
        arrays[name] = np.ascontiguousarray(inputs[f"L0_attn_{given}"])
    b1 = arrays["b1"].reshape(MOE_EXPERTS * HID_CHUNKS, P)
    arrays["b1"] = np.ascontiguousarray(b1.T)
    for name, given in FFN_PLAIN.items():
        arrays[name] = np.ascontiguousarray(inputs[f"L0_ffn_{given}"])
    for name, given in FFN_TURNED.items():
        arrays[name] = np.ascontiguousarray(np.asarray(inputs[f"L0_ffn_{given}"]).T)
    return arrays


def kernel(**inputs):
    import concourse.bacc as bacc
    from concourse.bass_utils import run_bass_kernel_spmd

    nc = bacc.Bacc("TRN2", target_bir_lowering=False, num_devices=1)
    arrays = host_arrays(inputs)
    w = {name: nc.dram_tensor(f"in_{name}", a.shape, mybir.dt.from_np(a.dtype), kind="ExternalInput").ap()
         for name, a in arrays.items()}
    x = w.pop("x")
    out = nc.dram_tensor("result", list(x.shape), F32, kind="ExternalOutput").ap()
    build(nc, w, x, out)
    got = run_bass_kernel_spmd(nc, [{f"in_{name}": a for name, a in arrays.items()}], core_ids=[0])
    return got.results[0]["result"]
```
